# Optimizing a Trainium2 kernel written in Bass

```python
import numpy as np
import jax
import jax.numpy as jnp

def _softmax(x, axis=-1):
    return jax.nn.softmax(x, axis=axis)

def _gelu(x):
    return jax.nn.gelu(x, approximate=True)

def _silu(x):
    return jax.nn.silu(x)

def _sigmoid(x):
    return jax.nn.sigmoid(x)

def _layernorm(x, axis=-1, eps=1e-05):
    m = jnp.mean(x, axis=axis, keepdims=True)
    v = jnp.var(x, axis=axis, keepdims=True)
    return (x - m) / jnp.sqrt(v + eps)

def _scatter_add(tgt, idx, src, axis=0):
    return tgt.at[idx].add(src)

def _segment_sum(src, seg, n):
    return jax.ops.segment_sum(src, seg, n)
kernel_name = 'mk_lm_tower_d2_tok_ids256_r4_342f4c'

def setup_inputs(seed: int=0):
    np.random.seed(seed)
    _w = jnp.asarray

    def _rec_inputs():
        import jax
        import jax.numpy as jnp
        _rk = jax.random.key(seed)
        x = jax.random.randint(jax.random.fold_in(_rk, 1), (32, 256), 0, 50257, jnp.int32)
        return x
    x = _rec_inputs()

    def _L0_tok_setup():
        import jax, jax.numpy as jnp
        import numpy as np
        VOCAB = 50257
        DIM = 64

        def _positional_table(seq_len, dim, dtype=jnp.float32):
            pos = jnp.arange(seq_len, dtype=dtype)[:, None]
            d = jnp.arange(dim)
            exponent = (d - d % 2).astype(dtype) / dim
            inv_freq = jnp.power(jnp.asarray(10000.0, dtype), -exponent)
            angle = pos * inv_freq
            return jnp.where(d % 2 == 0, jnp.sin(angle), jnp.cos(angle))
        key = jax.random.key(seed)
        k1, k2 = jax.random.split(key)
        x = jax.random.randint(k1, (32, 1024), 0, VOCAB)
        W = jax.random.normal(k2, (VOCAB, DIM), dtype=jnp.float32)
        return {'x': x, 'W': W}
    _L0_tok_all = _L0_tok_setup()
    _L0_tok_in = {k: v for k, v in _L0_tok_all.items() if k in ('W',)}
    del _L0_tok_all

    def _L0_attn_setup():
        import jax, jax.numpy as jnp
        from jax import lax
        import numpy as np
        DIM, DT_RANK, D_INNER, D_STATE = (64, 16, 64, 16)

        def _ssm_params(key, d, dt_rank, d_inner, n):
            k1, k2, k3 = jax.random.split(key, 3)
            Wdbc = jax.random.normal(k1, (d, dt_rank + 2 * n), jnp.float32) * 0.02
            Wdt = jax.random.normal(k2, (dt_rank, d_inner), jnp.float32) * 0.02
            bdt = jax.random.normal(k3, (d_inner,), jnp.float32) * 0.02
            Alog = jnp.log(jnp.tile(jnp.arange(1, n + 1, dtype=jnp.float32), (d_inner, 1)))
            D = jnp.ones((d_inner,), jnp.float32)
            return (Wdbc, Wdt, bdt, Alog, D)

        def _layernorm(x, g, b, eps=1e-05):
            mu = jnp.mean(x, -1, keepdims=True)
            var = jnp.var(x, -1, keepdims=True)
            return (x - mu) * lax.rsqrt(var + eps) * g + b

        def _selective_scan(x, delta, A, B, C, D):
            deltaA = jnp.exp(delta[..., None] * A)
            BX = delta[..., None] * B[:, :, None, :] * x[..., None]
            dA = jnp.moveaxis(deltaA, 1, 0)
            bx = jnp.moveaxis(BX, 1, 0)

            def step(h, inp):
                dA_t, bx_t = inp
                h = dA_t * h + bx_t
                return (h, h)
            h0 = jnp.zeros_like(dA[0])
            _, hs = lax.scan(step, h0, (dA, bx))
            hs = jnp.moveaxis(hs, 0, 1)
            y = jnp.einsum('bsdn,bsn->bsd', hs, C) + D * x
            return y

        def _ssm(x, Wdbc, Wdt, bdt, Alog, D):
            A = -jnp.exp(Alog)
            dbc = x @ Wdbc
            dt_r, B, C = jnp.split(dbc, [DT_RANK, DT_RANK + D_STATE], axis=-1)
            delta = jax.nn.softplus(dt_r @ Wdt + bdt)
            return _selective_scan(x, delta, A, B, C, D)

        def _process(x, Wc, bc, Wdbc, Wdt, bdt, Alog, D):
            x = jax.nn.softplus(x @ Wc.T + bc)
            return _ssm(x, Wdbc, Wdt, bdt, Alog, D)
        key = jax.random.key(seed)
        ks = jax.random.split(key, 10)
        x = jax.random.normal(ks[0], (4, 1024, DIM), jnp.float32)
        ln_g = jnp.ones((DIM,), jnp.float32)
        ln_b = jnp.zeros((DIM,), jnp.float32)
        Wp = jax.random.normal(ks[1], (DIM, DIM), jnp.float32) * 0.02
        bp = jnp.zeros((DIM,), jnp.float32)
        Wcf = jax.random.normal(ks[2], (DIM, DIM), jnp.float32) * 0.02
        bcf = jnp.zeros((DIM,), jnp.float32)
        Wcb = jax.random.normal(ks[3], (DIM, DIM), jnp.float32) * 0.02
        bcb = jnp.zeros((DIM,), jnp.float32)
        Wdbc_f, Wdt_f, bdt_f, Alog_f, D_f = _ssm_params(ks[4], DIM, DT_RANK, D_INNER, D_STATE)
        Wdbc_b, Wdt_b, bdt_b, Alog_b, D_b = _ssm_params(ks[5], DIM, DT_RANK, D_INNER, D_STATE)
        return dict(x=x, ln_g=ln_g, ln_b=ln_b, Wp=Wp, bp=bp, Wcf=Wcf, bcf=bcf, Wcb=Wcb, bcb=bcb, Wdbc_f=Wdbc_f, Wdt_f=Wdt_f, bdt_f=bdt_f, Alog_f=Alog_f, D_f=D_f, Wdbc_b=Wdbc_b, Wdt_b=Wdt_b, bdt_b=bdt_b, Alog_b=Alog_b, D_b=D_b)
    _L0_attn_all = _L0_attn_setup()
    _L0_attn_in = {k: v for k, v in _L0_attn_all.items() if k in ('ln_g', 'ln_b', 'Wp', 'bp', 'Wcf', 'bcf', 'Wcb', 'bcb', 'Wdbc_f', 'Wdt_f', 'bdt_f', 'Alog_f', 'D_f', 'Wdbc_b', 'Wdt_b', 'bdt_b', 'Alog_b', 'D_b')}
    del _L0_attn_all

    def _L0_ffn_setup():
        import jax, jax.numpy as jnp
        import numpy as np
        NUM_EXPERTS = 8
        TOP_K = 2
        B, S, D = (8, 2048, 64)

        def _moe(tokens, router_w, w1, b1, w2, b2):
            N = tokens.shape[0]
            E = router_w.shape[0]
            logits = tokens.astype(jnp.float32) @ router_w.astype(jnp.float32).T
            probs = jax.nn.softmax(logits, axis=-1)
            rw, re = jax.lax.top_k(probs, TOP_K)
            if TOP_K > 1:
                rw = rw / jnp.maximum(rw.sum(-1, keepdims=True), 1e-12)
            rw = rw.astype(tokens.dtype)
            combine = jnp.zeros((N, E), tokens.dtype).at[jnp.arange(N)[:, None], re].set(rw)
            out = tokens
            for e in range(E):
                h = jax.nn.gelu(tokens @ w1[e] + b1[e], approximate=False)
                y = h @ w2[e] + b2[e]
                out = out + combine[:, e:e + 1] * y
            return out
        key = jax.random.key(seed)
        ks = jax.random.split(key, 4)
        scale = 1.0 / np.sqrt(D).astype(np.float32)
        return {'input_embeddings': jax.random.normal(ks[0], (B, S, D), jnp.float32), 'router_w': jax.random.normal(ks[1], (NUM_EXPERTS, D), jnp.float32) * scale, 'w1': jax.random.normal(ks[2], (NUM_EXPERTS, D, D), jnp.float32) * scale, 'b1': jnp.zeros((NUM_EXPERTS, D), jnp.float32), 'w2': jax.random.normal(ks[3], (NUM_EXPERTS, D, D), jnp.float32) * scale, 'b2': jnp.zeros((NUM_EXPERTS, D), jnp.float32)}
    _L0_ffn_all = _L0_ffn_setup()
    _L0_ffn_in = {k: v for k, v in _L0_ffn_all.items() if k in ('router_w', 'w1', 'b1', 'w2', 'b2')}
    del _L0_ffn_all

    def _L1_attn_setup():
        import jax, jax.numpy as jnp
        import numpy as np
        H, D = (8, 32)
        EPS = 1e-05
        key = jax.random.key(seed)
        ks = jax.random.split(key, 4)
        B, N, C = (2, 512, 64)
        inner = H * D
        return {'node_features': jax.random.normal(ks[0], (B, N, C), jnp.float32), 'ln_gamma': jnp.ones((C,), jnp.float32), 'ln_beta': jnp.zeros((C,), jnp.float32), 'W_qkv': jax.random.normal(ks[1], (3 * inner, C), jnp.float32) * 0.02, 'W_gate': jax.random.normal(ks[2], (inner, C), jnp.float32) * 0.02, 'b_gate': jnp.ones((inner,), jnp.float32), 'W_final': jax.random.normal(ks[3], (C, inner), jnp.float32) * 0.02, 'b_final': jnp.zeros((C,), jnp.float32)}
    _L1_attn_all = _L1_attn_setup()
    _L1_attn_in = {k: v for k, v in _L1_attn_all.items() if k in ('ln_gamma', 'ln_beta', 'W_qkv', 'W_gate', 'b_gate', 'W_final', 'b_final')}
    del _L1_attn_all

    def _L1_ffn_setup():
        import jax, jax.numpy as jnp
        import numpy as np
        B, H, E, IN, OUT = (1024, 1, 8, 64, 64)

        @jax.custom_vjp
        def bin_active(x):
            return jnp.sign(x)

        def _ba_fwd(x):
            return (jnp.sign(x), x)

        def _ba_bwd(x, g):
            return (g * (jnp.abs(x) <= 1.0).astype(g.dtype),)
        bin_active.defvjp(_ba_fwd, _ba_bwd)

        @jax.custom_vjp
        def bin_gate(x):
            return (x > 0.5).astype(x.dtype)

        def _bg_fwd(x):
            return ((x > 0.5).astype(x.dtype), None)

        def _bg_bwd(_, g):
            return (g,)
        bin_gate.defvjp(_bg_fwd, _bg_bwd)
        key = jax.random.key(seed)
        k1, k2, k3, k4, k5 = jax.random.split(key, 5)
        x = jax.random.normal(k1, (B, H, IN), dtype=jnp.float32)
        weight = jax.random.normal(k2, (H, E, IN, OUT), dtype=jnp.float32) * 0.05
        proj_w = jax.random.normal(k3, (E, IN), dtype=jnp.float32) * 0.05
        proj_b = jax.random.normal(k4, (E,), dtype=jnp.float32) * 0.05
        scale = jax.random.normal(k5, (H, 1, OUT), dtype=jnp.float32) * 0.1
        return {'x': x, 'weight': weight, 'proj_w': proj_w, 'proj_b': proj_b, 'scale': scale}
    _L1_ffn_all = _L1_ffn_setup()
    _L1_ffn_in = {k: v for k, v in _L1_ffn_all.items() if k in ('weight', 'proj_w', 'proj_b', 'scale')}
    del _L1_ffn_all
    return {'x': x, 'L0_tok_W': _L0_tok_in['W'], 'L0_attn_ln_g': _L0_attn_in['ln_g'], 'L0_attn_ln_b': _L0_attn_in['ln_b'], 'L0_attn_Wp': _L0_attn_in['Wp'], 'L0_attn_bp': _L0_attn_in['bp'], 'L0_attn_Wcf': _L0_attn_in['Wcf'], 'L0_attn_bcf': _L0_attn_in['bcf'], 'L0_attn_Wcb': _L0_attn_in['Wcb'], 'L0_attn_bcb': _L0_attn_in['bcb'], 'L0_attn_Wdbc_f': _L0_attn_in['Wdbc_f'], 'L0_attn_Wdt_f': _L0_attn_in['Wdt_f'], 'L0_attn_bdt_f': _L0_attn_in['bdt_f'], 'L0_attn_Alog_f': _L0_attn_in['Alog_f'], 'L0_attn_D_f': _L0_attn_in['D_f'], 'L0_attn_Wdbc_b': _L0_attn_in['Wdbc_b'], 'L0_attn_Wdt_b': _L0_attn_in['Wdt_b'], 'L0_attn_bdt_b': _L0_attn_in['bdt_b'], 'L0_attn_Alog_b': _L0_attn_in['Alog_b'], 'L0_attn_D_b': _L0_attn_in['D_b'], 'L0_ffn_router_w': _L0_ffn_in['router_w'], 'L0_ffn_w1': _L0_ffn_in['w1'], 'L0_ffn_b1': _L0_ffn_in['b1'], 'L0_ffn_w2': _L0_ffn_in['w2'], 'L0_ffn_b2': _L0_ffn_in['b2'], 'L1_attn_ln_gamma': _L1_attn_in['ln_gamma'], 'L1_attn_ln_beta': _L1_attn_in['ln_beta'], 'L1_attn_W_qkv': _L1_attn_in['W_qkv'], 'L1_attn_W_gate': _L1_attn_in['W_gate'], 'L1_attn_b_gate': _L1_attn_in['b_gate'], 'L1_attn_W_final': _L1_attn_in['W_final'], 'L1_attn_b_final': _L1_attn_in['b_final'], 'L1_ffn_weight': _L1_ffn_in['weight'], 'L1_ffn_proj_w': _L1_ffn_in['proj_w'], 'L1_ffn_proj_b': _L1_ffn_in['proj_b'], 'L1_ffn_scale': _L1_ffn_in['scale']}

def reference(x, L0_tok_W, L0_attn_ln_g, L0_attn_ln_b, L0_attn_Wp, L0_attn_bp, L0_attn_Wcf, L0_attn_bcf, L0_attn_Wcb, L0_attn_bcb, L0_attn_Wdbc_f, L0_attn_Wdt_f, L0_attn_bdt_f, L0_attn_Alog_f, L0_attn_D_f, L0_attn_Wdbc_b, L0_attn_Wdt_b, L0_attn_bdt_b, L0_attn_Alog_b, L0_attn_D_b, L0_ffn_router_w, L0_ffn_w1, L0_ffn_b1, L0_ffn_w2, L0_ffn_b2, L1_attn_ln_gamma, L1_attn_ln_beta, L1_attn_W_qkv, L1_attn_W_gate, L1_attn_b_gate, L1_attn_W_final, L1_attn_b_final, L1_ffn_weight, L1_ffn_proj_w, L1_ffn_proj_b, L1_ffn_scale):
    import jax
    import jax.numpy as jnp

    def _L0_tok_ref(x, W):
        import jax, jax.numpy as jnp
        import numpy as np
        VOCAB = 50257
        DIM = 64

        def _positional_table(seq_len, dim, dtype=jnp.float32):
            pos = jnp.arange(seq_len, dtype=dtype)[:, None]
            d = jnp.arange(dim)
            exponent = (d - d % 2).astype(dtype) / dim
            inv_freq = jnp.power(jnp.asarray(10000.0, dtype), -exponent)
            angle = pos * inv_freq
            return jnp.where(d % 2 == 0, jnp.sin(angle), jnp.cos(angle))
        seq_len = x.shape[1]
        pe = _positional_table(seq_len, W.shape[1], W.dtype)
        return W[x] + pe[None, :, :]

    def _L0_attn_ref(x, ln_g, ln_b, Wp, bp, Wcf, bcf, Wcb, bcb, Wdbc_f, Wdt_f, bdt_f, Alog_f, D_f, Wdbc_b, Wdt_b, bdt_b, Alog_b, D_b):
        import jax, jax.numpy as jnp
        from jax import lax
        import numpy as np
        DIM, DT_RANK, D_INNER, D_STATE = (64, 16, 64, 16)

        def _ssm_params(key, d, dt_rank, d_inner, n):
            k1, k2, k3 = jax.random.split(key, 3)
            Wdbc = jax.random.normal(k1, (d, dt_rank + 2 * n), jnp.float32) * 0.02
            Wdt = jax.random.normal(k2, (dt_rank, d_inner), jnp.float32) * 0.02
            bdt = jax.random.normal(k3, (d_inner,), jnp.float32) * 0.02
            Alog = jnp.log(jnp.tile(jnp.arange(1, n + 1, dtype=jnp.float32), (d_inner, 1)))
            D = jnp.ones((d_inner,), jnp.float32)
            return (Wdbc, Wdt, bdt, Alog, D)

        def _layernorm(x, g, b, eps=1e-05):
            mu = jnp.mean(x, -1, keepdims=True)
            var = jnp.var(x, -1, keepdims=True)
            return (x - mu) * lax.rsqrt(var + eps) * g + b

        def _selective_scan(x, delta, A, B, C, D):
            deltaA = jnp.exp(delta[..., None] * A)
            BX = delta[..., None] * B[:, :, None, :] * x[..., None]
            dA = jnp.moveaxis(deltaA, 1, 0)
            bx = jnp.moveaxis(BX, 1, 0)

            def step(h, inp):
                dA_t, bx_t = inp
                h = dA_t * h + bx_t
                return (h, h)
            h0 = jnp.zeros_like(dA[0])
            _, hs = lax.scan(step, h0, (dA, bx))
            hs = jnp.moveaxis(hs, 0, 1)
            y = jnp.einsum('bsdn,bsn->bsd', hs, C) + D * x
            return y

        def _ssm(x, Wdbc, Wdt, bdt, Alog, D):
            A = -jnp.exp(Alog)
            dbc = x @ Wdbc
            dt_r, B, C = jnp.split(dbc, [DT_RANK, DT_RANK + D_STATE], axis=-1)
            delta = jax.nn.softplus(dt_r @ Wdt + bdt)
            return _selective_scan(x, delta, A, B, C, D)

        def _process(x, Wc, bc, Wdbc, Wdt, bdt, Alog, D):
            x = jax.nn.softplus(x @ Wc.T + bc)
            return _ssm(x, Wdbc, Wdt, bdt, Alog, D)
        skip = x
        xn = _layernorm(x, ln_g, ln_b)
        z1 = xn @ Wp + bp
        xp = z1
        x1 = jax.nn.silu(_process(xp, Wcf, bcf, Wdbc_f, Wdt_f, bdt_f, Alog_f, D_f))
        x2r = _process(jnp.flip(xp, 1), Wcb, bcb, Wdbc_b, Wdt_b, bdt_b, Alog_b, D_b)
        x2 = jax.nn.silu(jnp.flip(x2r, 1))
        z = jax.nn.silu(z1)
        return x1 * z + x2 * z + skip

    def _L0_ffn_ref(input_embeddings, router_w, w1, b1, w2, b2):
        import jax, jax.numpy as jnp
        import numpy as np
        NUM_EXPERTS = 8
        TOP_K = 2
        B, S, D = (8, 2048, 64)

        def _moe(tokens, router_w, w1, b1, w2, b2):
            N = tokens.shape[0]
            E = router_w.shape[0]
            logits = tokens.astype(jnp.float32) @ router_w.astype(jnp.float32).T
            probs = jax.nn.softmax(logits, axis=-1)
            rw, re = jax.lax.top_k(probs, TOP_K)
            if TOP_K > 1:
                rw = rw / jnp.maximum(rw.sum(-1, keepdims=True), 1e-12)
            rw = rw.astype(tokens.dtype)
            combine = jnp.zeros((N, E), tokens.dtype).at[jnp.arange(N)[:, None], re].set(rw)
            out = tokens
            for e in range(E):
                h = jax.nn.gelu(tokens @ w1[e] + b1[e], approximate=False)
                y = h @ w2[e] + b2[e]
                out = out + combine[:, e:e + 1] * y
            return out
        b, s, d = input_embeddings.shape
        tokens = input_embeddings.reshape(b * s, d)
        return _moe(tokens, router_w, w1, b1, w2, b2).reshape(b, s, d)

    def _L1_attn_ref(node_features, ln_gamma, ln_beta, W_qkv, W_gate, b_gate, W_final, b_final):
        import jax, jax.numpy as jnp
        import numpy as np
        H, D = (8, 32)
        EPS = 1e-05
        x = node_features
        B, N, _ = x.shape
        mu = jnp.mean(x, axis=-1, keepdims=True)
        var = jnp.mean(jnp.square(x - mu), axis=-1, keepdims=True)
        normed = (x - mu) / jnp.sqrt(var + EPS) * ln_gamma + ln_beta
        qkv = normed @ W_qkv.T
        q, k, v = jnp.split(qkv, 3, axis=-1)

        def to_heads(t):
            return t.reshape(B, N, H, D).transpose(0, 2, 1, 3)
        q, k, v = (to_heads(q), to_heads(k), to_heads(v))
        gate = jax.nn.sigmoid(to_heads(x @ W_gate.T + b_gate))
        scores = jnp.einsum('bhid,bhjd->bhij', q, k) * D ** (-0.5)
        attn = jax.nn.softmax(scores, axis=-1)
        out = jnp.einsum('bhij,bhid->bhjd', attn, v) * gate
        out = out.transpose(0, 2, 1, 3).reshape(B, N, H * D)
        return x + out @ W_final.T + b_final

    def _L1_ffn_ref(x, weight, proj_w, proj_b, scale):
        import jax, jax.numpy as jnp
        import numpy as np
        B, H, E, IN, OUT = (1024, 1, 8, 64, 64)

        @jax.custom_vjp
        def bin_active(x):
            return jnp.sign(x)

        def _ba_fwd(x):
            return (jnp.sign(x), x)

        def _ba_bwd(x, g):
            return (g * (jnp.abs(x) <= 1.0).astype(g.dtype),)
        bin_active.defvjp(_ba_fwd, _ba_bwd)

        @jax.custom_vjp
        def bin_gate(x):
            return (x > 0.5).astype(x.dtype)

        def _bg_fwd(x):
            return ((x > 0.5).astype(x.dtype), None)

        def _bg_bwd(_, g):
            return (g,)
        bin_gate.defvjp(_bg_fwd, _bg_bwd)
        xh = jnp.transpose(x, (1, 0, 2))
        gate = jax.nn.sigmoid(jnp.einsum('hbi,ei->hbe', xh, proj_w) + proj_b)
        gate = bin_gate(gate)
        w = jnp.einsum('hbe,heio->hbio', gate, weight)
        xb = bin_active(xh)
        wb = bin_active(w)
        y = jnp.einsum('hbi,hbio->hbo', xb, wb)
        y = y * scale
        return jnp.transpose(y, (1, 0, 2))
    h = _L0_tok_ref(x, L0_tok_W)
    h = h + _L0_attn_ref(_layernorm(h, axis=-1), L0_attn_ln_g, L0_attn_ln_b, L0_attn_Wp, L0_attn_bp, L0_attn_Wcf, L0_attn_bcf, L0_attn_Wcb, L0_attn_bcb, L0_attn_Wdbc_f, L0_attn_Wdt_f, L0_attn_bdt_f, L0_attn_Alog_f, L0_attn_D_f, L0_attn_Wdbc_b, L0_attn_Wdt_b, L0_attn_bdt_b, L0_attn_Alog_b, L0_attn_D_b)
    h = h + _L0_ffn_ref(_layernorm(h, axis=-1), L0_ffn_router_w, L0_ffn_w1, L0_ffn_b1, L0_ffn_w2, L0_ffn_b2)
    h = h + _L1_attn_ref(_layernorm(h, axis=-1), L1_attn_ln_gamma, L1_attn_ln_beta, L1_attn_W_qkv, L1_attn_W_gate, L1_attn_b_gate, L1_attn_W_final, L1_attn_b_final)
    h = h + _L1_ffn_ref(_layernorm(h, axis=-1), L1_ffn_weight, L1_ffn_proj_w, L1_ffn_proj_b, L1_ffn_scale)
    return h

_drawn_inputs = setup_inputs


def setup_inputs(seed=0):
    import zlib

    import numpy as np

    out = dict(_drawn_inputs(seed))
    spreads = {'L0_attn_ln_g': (1.0, 0.2),
     'L0_attn_ln_b': (0.0, 0.355),
     'L0_attn_bp': (0.0, 0.1),
     'L0_attn_bcf': (0.0, 0.557),
     'L0_attn_bcb': (0.0, 0.569),
     'L0_attn_D_f': (1.0, 0.6),
     'L0_attn_D_b': (1.0, 0.6),
     'L0_ffn_b1': (0.0, 0.1),
     'L0_ffn_b2': (0.0, 0.1),
     'L1_attn_ln_gamma': (1.0, 0.6),
     'L1_attn_ln_beta': (0.0, 0.8),
     'L1_attn_b_gate': (1.0, 0.6),
     'L1_attn_b_final': (0.0, 0.1)}
    factors = {'L0_attn_Wcf': 8.0,
     'L0_attn_Wcb': 8.0,
     'L0_attn_Wdbc_f': 8.0,
     'L0_attn_Wdt_f': 8.0,
     'L0_attn_bdt_f': 31.669,
     'L0_attn_Alog_f': 8.0,
     'L0_attn_Wdbc_b': 6.316,
     'L0_attn_Wdt_b': 8.0,
     'L0_attn_bdt_b': 8.0,
     'L0_attn_Alog_b': 8.0,
     'L1_attn_W_qkv': 3.821,
     'L1_attn_W_gate': 8.0,
     'L1_attn_W_final': 3.855}
    for name, (base, spread) in spreads.items():
        noise = np.random.default_rng([zlib.crc32(name.encode()), seed]).standard_normal(out[name].shape)
        drawn = base * np.exp(spread * noise) if base else spread * noise
        out[name] = jnp.asarray(drawn.astype(out[name].dtype))
    for name, factor in factors.items():
        out[name] = (out[name] * factor).astype(out[name].dtype)
    return out
```

```python
from contextlib import ExitStack

import concourse.bass as bass
from concourse import mybir

F32 = mybir.dt.float32
BF16 = mybir.dt.bfloat16
I32 = mybir.dt.int32
U16 = mybir.dt.uint16
ALU = mybir.AluOpType
ACT = mybir.ActivationFunctionType
AX = mybir.AxisListType

P = 128
D = 64
SEQ = 256
BATCH = 32
GROUPS = 8
N = 512
TILES = 8
STATES = 16
DT_RANK = 16
EXPERTS = 8
HEADS = 8
HEAD_DIM = 32
EPS = 1e-5
SOFTPLUS_CAP = 40.0
RING = 3

_WIDTHS = [
    ("ident", 128), ("perm", 128), ("Wp", 128), ("Wc", 256), ("Wx", 4 * 96), ("dt_in", 128), ("dt_out", 256),
    ("dt_in_b", 128), ("W1", 8 * 128), ("W2", 4 * 64), ("b2", 128), ("router", 16), ("Wq", 512), ("Wk", 512),
    ("Wv", 512), ("Wg", 512), ("Wf", 128), ("proj", 96), ("pe", 512), ("iota", 64), ("mhalf", 8), ("eps64", 8), ("eps", 8),
    ("ln_g", 1), ("ln_b", 1), ("bp", 1), ("bc", 2), ("bdt", 2), ("Dskip", 2), ("Alog", 32), ("b1", 4),
    ("gamma", 1), ("beta", 1), ("bg", 2), ("bf", 1), ("scale", 1), ("pb", 1), ("n1", 1), ("n2", 1),
    ("w_n1", 1), ("w_n2", 1), ("w_s", 2),
]
COL, _at = {}, 0
for _name, _w in _WIDTHS:
    COL[_name] = (_at, _w)
    _at += _w
NCONST = _at


class Signal:

    def __init__(self, sem, per, seed=0):
        self.sem, self.per, self.seed = sem, per, seed

    def __call__(self, g, k):
        return self.sem, g * self.per + (k + self.seed)


def bcast(ap, n):
    p, m = ap.shape
    return ap.unsqueeze(2).to_broadcast([p, m, n])


def build_tower(nc, table, ids, consts, selectors, ones_sel, w_exp, out):
    with ExitStack() as ctx:
        def sb(name, shape, dt=F32):
            return ctx.enter_context(nc.sbuf_tensor(name, shape, dt))

        signals = {}

        def sig(name, per, seed=0):
            s = Signal(ctx.enter_context(nc.semaphore(name)), per, seed)
            signals[name] = s
            return s

        cst = sb("cst", [P, NCONST])

        def C(name, i=0, w=None, rows=P):
            at, width = COL[name]
            w = width if w is None else w
            return cst[0:rows, at + i * w:at + (i + 1) * w]

        ident = C("ident")
        sel = sb("sel", [96, STATES, P], BF16)
        ones_w = sb("ones_w", [P, 16, 32], BF16)
        Wt = sb("Wt", [96, D, P], BF16)
        idx_all = sb("idx_all", [P, (GROUPS + 1) * TILES], I32)
        idx = sb("idx", [P, TILES], I32)
        negA = sb("negA", [P, 2 * STATES])
        Wdt = sb("Wdt", [P, 2, P])
        half_bg = sb("half_bg", [P, 2])
        half_Wf = sb("half_Wf", [P, 2, D])

        emb = sb("emb", [P, N])
        hM = sb("hM", [P, N])
        hB = sb("hB", [P, N])
        xcM, sqM = sb("xcM", [P, N]), sb("sqM", [P, N])
        xlM, xnM = sqM, xcM
        stM = sb("stM", [P, 8, TILES])
        xnF = sb("xnF", [P, N])
        z1 = sb("z1", [P, N])
        um = sb("um", [P, 2, N])
        u = sb("u", [P, 2, N])
        hi = sb("hi", [96, 2 * N], BF16)
        r1 = um[0:96, :, :].rearrange("p j n -> p (j n)")
        mid = sb("mid", [96, 2 * N], BF16)
        SX = sb("SX", [96, 2, 2 * N], BF16)
        delta = sb("delta", [P, 2, N])
        du = sb("du", [P, 2, N])
        dA = sb("dA", [P, 2, RING, N])
        bx = sb("bx", [P, 2, N])
        hs = sb("hs", [P, 2, N])
        pC = sb("pC", [P, RING, N])
        acc = sb("acc", [P, 2, N])
        th, sy, mF = pC, bx, hs[:, 0, :]

        hR = sb("hR", [P, N])
        xcR, sqR = sb("xcR", [P, N]), sb("sqR", [P, N])
        xR, xnR = sqR, xcR
        stR = sb("stR", [P, 8, TILES])
        aF = sb("aF", [P, N])
        nF = sb("nF", [P, N])
        oF = aF
        rt = sb("rt", [P, 8, TILES * EXPERTS])
        rs8 = sb("rs8", [P, 10, TILES])
        comb = sb("comb", [P, TILES * EXPERTS])
        cT = sb("cT", [16, N])
        qF = sb("qF", [P, 4, N])
        ge, gg = qF[:, 0:2, :], qF[:, 2:4, :]
        kF = sb("kF", [P, 4, N])
        kz = sb("kz", [P, 16, N])
        vT = sb("vT", [P, 4, N])
        thg = sb("thg", [P, 4, N])
        nmx = sb("nmx", [P, 4, 2])
        rsum = sb("rsum", [P, 4, 2])
        rinv = sb("rinv", [P, 4, 2])
        prob = sb("prob", [P, RING, 2, SEQ])
        vs = sb("vs", [P, RING, 2, HEAD_DIM])
        og = thg
        xb = sb("xb", [P, N], BF16)
        G = sb("G", [96, N], BF16)
        sg = kF[:, 0:2, :].rearrange("p j n -> p (j n)").bitcast(BF16).rearrange("p (j n) -> p j n", n=N)
        zz = kF[:, 2:4, :].rearrange("p j n -> p (j n)").bitcast(BF16).rearrange("p (j n) -> p j n", n=N)
        outT = sb("outT", [P, N])

        ps = [ctx.enter_context(nc.psum_tensor(f"ps{i}", [P, N], F32)) for i in range(4)]
        bank4 = ctx.enter_context(nc.psum_tensor("psR", [P, 4, N], F32))
        rb = [bank4[:, i, :] for i in range(4)]
        loaded = sig("loaded", 0)
        prepared = sig("prepared", 0)
        emb_landed = sig("emb_landed", 16 * TILES)
        idx_copied = sig("idx_copied", 1)
        emb_used = sig("emb_used", 1)
        v_chain = sig("v_chain", 0)
        ln_xc = [sig(f"ln_xc{i}", 1) for i in range(4)]
        ln_sq = [sig(f"ln_sq{i}", 1) for i in range(4)]
        ln_var = [sig(f"ln_var{i}", 1) for i in range(4)]
        ln_rs = [sig(f"ln_rs{i}", 6 if i in (0, 2) else 2) for i in range(4)]
        xn_ready = sig("xn_ready", 1)
        xnT_ready = sig("xnT_ready", 1)
        xnF_ready = sig("xnF_ready", 1)
        z1p_ready = sig("z1p_ready", 1)
        z1_ready = sig("z1_ready", 1)
        upre_ready = sig("upre_ready", 2)
        um_ready = sig("um_ready", 4)
        se_ready = sig("se_ready", 4)
        sl_ready = sig("sl_ready", 4)
        u_ready = sig("u_ready", 2)
        xp_ready = sig("xp_ready", 2)
        hi_ready = sig("hi_ready", 2)
        r1_ready = sig("r1_ready", 2)
        mid_ready = sig("mid_ready", 2)
        sx_ready = sig("sx_ready", 2)
        dpre_ready = sig("dpre_ready", 2)
        delta_ready = sig("delta_ready", 2)
        du_ready = sig("du_ready", 2)
        acc_init = sig("acc_init", 2)
        b_ready = sig("b_ready", 2 * STATES)
        c_ready = sig("c_ready", 2 * STATES)
        dA_ready = sig("dA_ready", 2 * STATES)
        bx_done = sig("bx_done", 2 * STATES)
        h_done = sig("h_done", 2 * STATES)
        p_done = sig("p_done", 2 * STATES)
        acc_done = sig("acc_done", 2 * STATES)
        th_ready = sig("th_ready", 3)
        m_ready = sig("m_ready", 1)
        mT_ready = sig("mT_ready", 1)
        h1_ready = sig("h1_ready", 1)

        xm_ready = sig("xm_ready", 1)
        xmT_ready = sig("xmT_ready", 1)
        xmF_ready = sig("xmF_ready", 1)
        lg_ready = sig("lg_ready", 1)
        ls_ready = sig("ls_ready", 1)
        le_ready = sig("le_ready", 1)
        comb_ready = sig("comb_ready", 1)
        cTp_ready = sig("cTp_ready", 1)
        cT_ready = sig("cT_ready", 1)
        hp_ready = sig("hp_ready", 8)
        cb_ready = sig("cb_ready", 8)
        ge_ready = sig("ge_ready", 8)
        gg_ready = sig("gg_ready", 8)
        mo_mm = sig("mo_mm", 8)
        moF_ready = sig("moF_ready", 1)
        moT_ready = sig("moT_ready", 1)
        xa_ready = sig("xa_ready", 2)
        xaT_ready = sig("xaT_ready", 2)
        xaF_ready = sig("xaF_ready", 2)
        pj_ready = sig("pj_ready", 16)
        pjA_done = sig("pjA_done", 12)
        pjV_done = sig("pjV_done", 4)
        kz_landed = sig("kz_landed", 16 * 16)
        sc_ready = sig("sc_ready", 32)
        nmx_ready = sig("nmx_ready", 32)
        exp_done = sig("exp_done", 64)
        rinv_ready = sig("rinv_ready", 32)
        vs_ready = sig("vs_ready", 32)
        ot_done = sig("ot_done", 32)
        og_ready = sig("og_ready", 4)
        fo_ready = sig("fo_ready", 1)
        foF_ready = sig("foF_ready", 1)
        foT_ready = sig("foT_ready", 1)
        xf_ready = sig("xf_ready", 1)
        xfT_ready = sig("xfT_ready", 1)
        xfF_ready = sig("xfF_ready", 2)
        gp_ready = sig("gp_ready", 1)
        G_ready = sig("G_ready", 1)
        w_ready = sig("w_ready", D)
        sg_ready = sig("sg_ready", D)
        zz_ready = sig("zz_ready", D)
        red_done = sig("red_done", D)
        yF_ready = sig("yF_ready", 1)
        yT_ready = sig("yT_ready", 1)
        out_ready = sig("out_ready", 1)
        stored = sig("stored", 16, seed=16)

        V_CHAIN = 33
        v_chain.per = V_CHAIN

        LOADS = 5
        PREP_V = 3 + 3 + 8 * 6 + 1
        PREPARED = 1 + 1 + PREP_V

        block = ctx.enter_context(nc.Block())

        @block.sync
        def _(sp):
            sp.dma_start(idx_all[:, :], ids).then_inc(loaded.sem, 16)
            sp.dma_start(cst[:, :], consts).then_inc(loaded.sem, 16)
            sp.dma_start(sel[:, :, :].bitcast(U16), selectors).then_inc(loaded.sem, 16)
            sp.dma_start(ones_w[:, :, :].bitcast(U16), ones_sel).then_inc(loaded.sem, 16)
            sp.dma_start(kz[0:96, 0:8, :], w_exp).then_inc(loaded.sem, 16)
            sp.sem_inc(stored.sem, 16)
            with sp.Fori(0, GROUPS) as g:
                for i in range(4):
                    sp.wait_ge(*pjA_done(g, 4 + 4 + i + 1))
                    for r in range(4):
                        rows = slice(32 * r, 32 * r + 32)
                        sp.dma_start(kz[rows, 4 * i + r, :], kF[rows, i, :]).then_inc(kz_landed.sem, 16)
                sp.wait_ge(*out_ready(g, 1))
                sp.dma_start(out[bass.ts(g, P), :], outT[:, :]).then_inc(stored.sem, 16)
            sp.wait_ge(*stored(GROUPS, 0))
            sp.wait_ge(*emb_landed(GROUPS + 1, 0))

        @block.gpsimd
        def _(pool):
            def gather():
                for k in range(TILES):
                    pool.indirect_dma_start(emb[:, k * D:(k + 1) * D], None, table,
                                            bass.IndirectOffsetOnAxis(ap=idx[:, k:k + 1], axis=0)
                                            ).then_inc(emb_landed.sem, 16)

            def root(g, i, st):
                var, rs, t, v2, r2 = (st[:, j, :] for j in range(1, 6))
                done = ln_rs[i]
                pool.wait_ge(*ln_var[i](g, 1))
                pool.tensor_tensor(t, var, C("eps64"), ALU.add).then_inc(done.sem, 1)
                pool.wait_ge(*done(g, 1))
                pool.tensor_tensor(rs, t, C("mhalf"), ALU.pow).then_inc(done.sem, 1)
                if done.per == 6:
                    pool.wait_ge(*done(g, 2))
                    pool.tensor_tensor(t, rs, rs, ALU.mult).then_inc(done.sem, 1)
                    pool.wait_ge(*done(g, 3))
                    pool.tensor_tensor(v2, t, var, ALU.mult).then_inc(done.sem, 1)
                    pool.wait_ge(*done(g, 4))
                    pool.tensor_tensor(v2, v2, C("eps"), ALU.add).then_inc(done.sem, 1)
                    pool.wait_ge(*done(g, 5))
                    pool.tensor_tensor(r2, v2, C("mhalf"), ALU.pow).then_inc(done.sem, 1)

            pool.wait_ge(loaded.sem, 16 * LOADS)
            pool.tensor_copy(idx[:, :], idx_all[:, 0:TILES]).then_inc(idx_copied.sem, 1)
            pool.wait_ge(idx_copied.sem, 1)
            gather()
            with pool.Fori(0, GROUPS) as g:
                pool.wait_ge(*emb_landed(g, 16 * TILES))
                pool.wait_ge(*emb_used(g, 1))
                pool.tensor_copy(idx[:, :], idx_all[:, bass.ds(g * TILES + TILES, TILES)]).then_inc(idx_copied.sem, 1)
                pool.wait_ge(*idx_copied(g, 2))
                root(g, 0, stM)
                gather()
                for d in range(2):
                    pool.wait_ge(*acc_init(g, d + 1))
                    for n in range(STATES):
                        k = d * STATES + n
                        pool.wait_ge(*p_done(g, k + 1))
                        if n:
                            pool.wait_ge(*acc_done(g, k))
                        pool.tensor_tensor(acc[:, d, :], acc[:, d, :], pC[:, k % RING, :], ALU.add
                                           ).then_inc(acc_done.sem, 1)
                for i in range(1, 4):
                    root(g, i, stR)

        @block.tensor
        def _(pe):
            def flip(dst, src):
                for k in range(4):
                    i = pe.transpose(dst[:, k * P:(k + 1) * P], src[:, k * P:(k + 1) * P], ident)
                return i

            def mm(dst, lhsT, rhs, start=True, stop=True):
                return pe.matmul(dst, lhsT, rhs, start=start, stop=stop)

            def scan_inputs(g):
                pe.wait_ge(*xn_ready(g, 1))
                flip(ps[0][:, :], xnM[:, :]).then_inc(xnT_ready.sem, 1)
                pe.wait_ge(*xnF_ready(g, 1))
                mm(ps[1][:, :], C("Wp"), xnF[:, :]).then_inc(z1p_ready.sem, 1)
                pe.wait_ge(*z1_ready(g, 1))
                for d in range(2):
                    mm(ps[2 + d][:, :], C("Wc", d, 128), z1[:, :]).then_inc(upre_ready.sem, 1)
                pe.wait_ge(*u_ready(g, 1))
                for d in range(2):
                    if d:
                        pe.wait_ge(*u_ready(g, 2))
                    mm(ps[2 * d][0:96, :], C("Wx", 2 * d, 96), u[:, d, :])
                    mm(ps[2 * d + 1][0:96, :], C("Wx", 2 * d + 1, 96), u[:, d, :]).then_inc(xp_ready.sem, 1)
                for d in range(2):
                    pe.wait_ge(*r1_ready(g, d + 1))
                    mm(ps[2 * d][:, :], Wdt[:, d, :], u[:, d, :]).then_inc(dpre_ready.sem, 1)

            def broadcast_b(g, k):
                d, n = divmod(k, STATES)
                if k >= 2:
                    pe.wait_ge(*bx_done(g, k - 1))
                if n == 0:
                    pe.wait_ge(*sx_ready(g, d + 1))
                mm(ps[k % 2][:, :], sel[:, n, :], SX[:, d, 0:N]).then_inc(b_ready.sem, 1)

            def broadcast_c(g, k):
                d, n = divmod(k, STATES)
                if k >= 2:
                    pe.wait_ge(*p_done(g, k - 1))
                mm(ps[2 + k % 2][:, :], sel[:, n, :], SX[:, d, N:2 * N]).then_inc(c_ready.sem, 1)

            def scan_states(g):
                pe.wait_ge(*delta_ready(g, 2))
                for k in range(2 * STATES):
                    broadcast_b(g, k)
                    broadcast_c(g, k)
                pe.wait_ge(*m_ready(g, 1))
                flip(ps[0][:, :], mF).then_inc(mT_ready.sem, 1)

            def experts(g):
                pe.wait_ge(*xm_ready(g, 1))
                flip(rb[0], xR[:, :]).then_inc(xmT_ready.sem, 1)
                pe.wait_ge(*xmF_ready(g, 1))
                for k in range(4):
                    i = mm(rb[1][:, k * 16:(k + 1) * 16], aF[:, k * P:(k + 1) * P], C("router"))
                i.then_inc(lg_ready.sem, 1)
                pe.wait_ge(*comb_ready(g, 1))
                for k in range(4):
                    i = mm(rb[2][0:16, k * P:(k + 1) * P], comb[:, k * 16:(k + 1) * 16], ident)
                i.then_inc(cTp_ready.sem, 1)
                pe.wait_ge(*cT_ready(g, 1))
                for s in range(2):
                    mm(rb[3][64 * s:64 * s + 64, :], C("b2", s, 64, 16), cT[:, :], True, False)

                def expert_out(v):
                    ep, s = divmod(v, 2)
                    pe.wait_ge(*gg_ready(g, v + 1))
                    mm(rb[3][64 * s:64 * s + 64, :], C("W2", ep, 64), gg[:, v % 2, :], False, ep == 3
                       ).then_inc(mo_mm.sem, 1)

                for v in range(8):
                    ep, s = divmod(v, 2)
                    if v >= 2:
                        pe.wait_ge(*ge_ready(g, v - 1))
                    mm(rb[v % 2], C("W1", 2 * ep + s, 128), aF[:, :]).then_inc(hp_ready.sem, 1)
                    if v:
                        pe.wait_ge(*gg_ready(g, v))
                    for k in range(4):
                        for e in range(2):
                            at = k * 16 + s * 8 + ep * 2 + e
                            i = mm(rb[2][64 * e:64 * e + 64, k * P:(k + 1) * P],
                                   comb[:, at:at + 1].to_broadcast([P, 64]), ident)
                    i.then_inc(cb_ready.sem, 1)
                    if v:
                        expert_out(v - 1)
                expert_out(7)
                pe.wait_ge(*moF_ready(g, 1))
                flip(rb[0], oF[:, :]).then_inc(moT_ready.sem, 1)

            def attention(g):
                pe.wait_ge(*xa_ready(g, 1))
                flip(rb[0], xR[:, :]).then_inc(xaT_ready.sem, 1)
                pe.wait_ge(*xa_ready(g, 2))
                flip(rb[1], xnR[:, :]).then_inc(xaT_ready.sem, 1)
                pe.wait_ge(*xaF_ready(g, 2))
                for w in range(16):
                    kind, i = divmod(w, 4)
                    if w >= RING:
                        if w - RING < 12:
                            pe.wait_ge(*pjA_done(g, w - RING + 1))
                        else:
                            pe.wait_ge(*pjV_done(g, w - RING - 12 + 1))
                    bank = rb[w % RING]
                    if kind < 3:
                        m = mm(bank, C(("Wg", "Wq", "Wk")[kind], i, 128), (aF if kind == 0 else nF)[:, :])
                    else:
                        s, a = divmod(i, 2)
                        for c in range(2):
                            at = (2 * a + c) * P
                            m = mm(bank[:, c * SEQ:(c + 1) * SEQ], nF[:, at:at + P], C("Wv", s, SEQ))
                    m.then_inc(pj_ready.sem, 1)
                pe.wait_ge(*kz_landed(g, 256))
                pe.wait_ge(*pjA_done(g, 12))
                pe.wait_ge(*pjV_done(g, 4))

                def scores(w):
                    sb_, a, r = w // 8, w // 4 % 2, w % 4
                    if w >= RING:
                        pe.wait_ge(*exp_done(g, 2 * (w - RING + 1)))
                    for c in range(2):
                        at = a * SEQ + c * P
                        m = mm(rb[w % RING][:, c * SEQ:(c + 1) * SEQ], qF[:, sb_, at:at + P],
                               kz[:, 4 * sb_ + r, a * SEQ:(a + 1) * SEQ])
                    m.then_inc(sc_ready.sem, 1)

                def weighted(w):
                    sb_, a, r = w // 8, w // 4 % 2, w % 4
                    if w % 8 == 0 and sb_:
                        pe.wait_ge(*og_ready(g, sb_))
                    pe.wait_ge(*vs_ready(g, w + 1))
                    for c in range(2):
                        m = mm(rb[3][32 * r:32 * r + 32, a * SEQ:(a + 1) * SEQ], vs[:, w % RING, c, :],
                               prob[:, w % RING, c, :], c == 0, c == 1)
                    m.then_inc(ot_done.sem, 1)

                for w in range(34):
                    if w < 32:
                        scores(w)
                    if w >= 2:
                        weighted(w - 2)
                for i in range(4):
                    s, b = divmod(i, 2)
                    pe.wait_ge(*og_ready(g, i + 1))
                    m = mm(rb[0][64 * s:64 * s + 64, :], half_Wf[:, b, :], og[:, i, :], b == 0, b == 1)
                m.then_inc(fo_ready.sem, 1)
                pe.wait_ge(*foF_ready(g, 1))
                flip(rb[1], oF[:, :]).then_inc(foT_ready.sem, 1)

            def binary(g):
                pe.wait_ge(*xf_ready(g, 1))
                flip(rb[0], xR[:, :]).then_inc(xfT_ready.sem, 1)
                pe.wait_ge(*xfF_ready(g, 2))
                mm(rb[1][0:96, :], C("proj"), aF[:, :]).then_inc(gp_ready.sem, 1)
                pe.wait_ge(*G_ready(g, 1))

                def expand(w):
                    if w >= RING:
                        pe.wait_ge(*sg_ready(g, w - RING + 1))
                    o = 16 * (w % 4) + w // 4
                    mm(rb[w % RING], Wt[:, o, :], G[:, :]).then_inc(w_ready.sem, 1)

                def reduce(w):
                    q, j = w % 4, w // 4
                    pe.wait_ge(*zz_ready(g, w + 1))
                    mm(rb[3][32 * q:32 * q + 32, :], ones_w[:, j, :], zz[:, w % RING, :], j == 0, j == 15
                       ).then_inc(red_done.sem, 1)

                for w in range(D + 2):
                    if w < D:
                        expand(w)
                    if w >= 2:
                        reduce(w - 2)
                pe.wait_ge(*yF_ready(g, 1))
                for k in range(4):
                    i = mm(rb[0][:, k * P:(k + 1) * P], oF[:, k * P:(k + 1) * P], C("perm"))
                i.then_inc(yT_ready.sem, 1)

            pe.wait_ge(loaded.sem, 16 * LOADS)
            mm(ps[0][:, 0:P], C("dt_in", 0, 128, 32), C("dt_out", 0, 128, 32))
            mm(ps[1][:, 0:P], C("dt_in_b", 0, 128, 32), C("dt_out", 1, 128, 32)).then_inc(prepared.sem, 1)
            pe.wait_ge(prepared.sem, PREPARED)
            with pe.Fori(0, GROUPS) as g:
                scan_inputs(g)
                scan_states(g)
                experts(g)
                attention(g)
                binary(g)

        @block.scalar
        def _(act):
            def square(g, i, dst, src):
                act.wait_ge(*ln_xc[i](g, 1))
                act.activation(dst, src, ACT.Square).then_inc(ln_sq[i].sem, 1)

            def softplus_log(g, i, buf):
                act.wait_ge(*um_ready(g, i + 1))
                act.activation(buf, um[:, i % 2, :], ACT.Exp).then_inc(se_ready.sem, 1)
                act.wait_ge(*se_ready(g, i + 1))
                act.activation(buf, buf, ACT.Ln, bias=1.0).then_inc(sl_ready.sem, 1)

            def scan_inputs(g):
                act.preload_act_table_set("natural_log_exp_and_others")
                square(g, 0, sqM[:, :], xcM[:, :])
                act.wait_ge(*xnT_ready(g, 1))
                act.activation(xnF[:, :], ps[0][:, :], ACT.Identity, bias=C("ln_b"), scale=C("ln_g")
                               ).then_inc(xnF_ready.sem, 1)
                act.wait_ge(*z1p_ready(g, 1))
                act.activation(z1[:, :], ps[1][:, :], ACT.Identity, bias=C("bp")).then_inc(z1_ready.sem, 1)
                for d in range(2):
                    softplus_log(g, d, um[:, d, :])
                for d in range(2):
                    act.wait_ge(*xp_ready(g, d + 1))
                    if d:
                        act.wait_ge(*r1_ready(g, 1))
                    for j in range(2):
                        i = act.activation(hi[:, j * N:(j + 1) * N], ps[2 * d + j][0:96, :], ACT.Copy)
                    i.then_inc(hi_ready.sem, 1)
                    act.wait_ge(*r1_ready(g, d + 1))
                    if d:
                        act.wait_ge(*sx_ready(g, 1))
                    act.activation(mid[:, :], r1, ACT.Copy).then_inc(mid_ready.sem, 1)
                for d in range(2):
                    softplus_log(g, 2 + d, um[:, d, :])

            def scan_states(g):
                for k in range(2 * STATES):
                    d, n = divmod(k, STATES)
                    if n == 0:
                        act.wait_ge(*delta_ready(g, d + 1))
                    if n >= RING:
                        act.wait_ge(*h_done(g, k - RING + 1))
                    cols = slice(1, SEQ) if d == 0 else slice(0, SEQ - 1)
                    src = delta[:, d, :].rearrange("p (a t) -> p a t", a=2)[:, :, cols]
                    dst = dA[:, d, k % RING, :].rearrange("p (a t) -> p a t", a=2)[:, :, cols]
                    act.activation(dst, src, ACT.Exp, scale=negA[:, k:k + 1]).then_inc(dA_ready.sem, 1)
                act.wait_ge(*acc_done(g, 2 * STATES))
                for d, src in enumerate((acc[:, 0, :], acc[:, 1, :], z1[:, :])):
                    act.activation(th[:, d, :], src, ACT.Tanh, scale=0.5).then_inc(th_ready.sem, 1)

            def experts(g):
                square(g, 1, sqR[:, :], xcR[:, :])
                act.wait_ge(*xmT_ready(g, 1))
                act.activation(aF[:, :], rb[0], ACT.Copy).then_inc(xmF_ready.sem, 1)
                act.wait_ge(*ls_ready(g, 1))
                act.activation(rt[:, 1, :], rt[:, 0, :], ACT.Exp).then_inc(le_ready.sem, 1)
                for v in range(8):
                    act.wait_ge(*hp_ready(g, v + 1))
                    if v >= 2:
                        act.wait_ge(*gg_ready(g, v - 1))
                    act.activation(ge[:, v % 2, :], rb[v % 2], ACT.Gelu, bias=C("b1", v // 2, 1)
                                   ).then_inc(ge_ready.sem, 1)
                act.wait_ge(*mo_mm(g, 8))
                act.activation(oF[:, :], rb[3], ACT.Copy).then_inc(moF_ready.sem, 1)

            def attention(g):
                square(g, 2, sqR[:, :], xcR[:, :])
                act.wait_ge(*xaT_ready(g, 1))
                act.activation(aF[:, :], rb[0], ACT.Copy).then_inc(xaF_ready.sem, 1)
                act.wait_ge(*xaT_ready(g, 2))
                act.activation(nF[:, :], rb[1], ACT.Identity, bias=C("beta"), scale=C("gamma")
                               ).then_inc(xaF_ready.sem, 1)
                for w in range(12):
                    kind, i = divmod(w, 4)
                    act.wait_ge(*pj_ready(g, w + 1))
                    if kind == 0:
                        m = act.activation(thg[:, i, :], rb[w % RING], ACT.Tanh, bias=half_bg[:, i % 2:i % 2 + 1],
                                           scale=0.5)
                    elif kind == 1:
                        m = act.activation(qF[:, i, :], rb[w % RING], ACT.Copy, scale=HEAD_DIM ** -0.5)
                    else:
                        m = act.activation(kF[:, i, :], rb[w % RING], ACT.Copy)
                    m.then_inc(pjA_done.sem, 1)
                for w in range(32):
                    act.wait_ge(*nmx_ready(g, w + 1))
                    if w >= RING:
                        act.wait_ge(*ot_done(g, w - RING + 1))
                    for c in range(2):
                        act.activation(prob[:, w % RING, c, :], rb[w % RING][:, c * SEQ:(c + 1) * SEQ], ACT.Exp,
                                       bias=nmx[:, w % 4, c:c + 1], accum_out=rsum[:, w % 4, c:c + 1]
                                       ).then_inc(exp_done.sem, 1)
                act.wait_ge(*fo_ready(g, 1))
                act.activation(oF[:, :], rb[0], ACT.Identity, bias=C("bf")).then_inc(foF_ready.sem, 1)

            def binary(g):
                square(g, 3, sqR[:, :], xcR[:, :])
                act.wait_ge(*xfT_ready(g, 1))
                act.activation(aF[:, :], rb[0], ACT.Copy).then_inc(xfF_ready.sem, 1)
                act.activation(xb[:, :], rb[0], ACT.Sign).then_inc(xfF_ready.sem, 1)
                for w in range(D):
                    act.wait_ge(*w_ready(g, w + 1))
                    if w >= RING:
                        act.wait_ge(*zz_ready(g, w - RING + 1))
                    act.activation(sg[:, w % RING, :], rb[w % RING], ACT.Sign).then_inc(sg_ready.sem, 1)
                act.wait_ge(*red_done(g, D))
                act.activation(oF[:, :], rb[3], ACT.Identity, bias=0.0, scale=C("scale")).then_inc(yF_ready.sem, 1)

            act.wait_ge(loaded.sem, 16 * LOADS)
            act.activation(negA[:, :], C("Alog"), ACT.Exp).then_inc(prepared.sem, 1)
            act.wait_ge(prepared.sem, PREPARED)
            with act.Fori(0, GROUPS) as g:
                scan_inputs(g)
                scan_states(g)
                experts(g)
                attention(g)
                binary(g)

        @block.vector
        def _(dve):
            tt, ts, stt, red = dve.tensor_tensor, dve.tensor_scalar, dve.scalar_tensor_tensor, dve.tensor_reduce
            step = [0]

            def link(g, ins):
                step[0] += 1
                ins.then_inc(v_chain.sem, 1)
                dve.wait_ge(*v_chain(g, step[0]))

            def tiles(ap):
                return ap.rearrange("p (k d) -> p k d", k=TILES)

            def layernorm(g, i, h, xc, sq, x, st, xn=None):
                s, var, rs, _, _, r2 = (st[:, j, :] for j in range(6))
                link(g, red(s, tiles(h), AX.X, ALU.add))
                stt(tiles(xc), bcast(s, D), -1.0 / D, tiles(h), ALU.mult, ALU.add).then_inc(ln_xc[i].sem, 1)
                dve.wait_ge(*ln_sq[i](g, 1))
                red(var, tiles(sq), AX.X, ALU.add).then_inc(ln_var[i].sem, 1)
                dve.wait_ge(*ln_rs[i](g, 2))
                out_x = stt(tiles(x), tiles(xc), float(D) ** 0.5, bcast(rs, D), ALU.mult, ALU.mult)
                if xn is None:
                    return out_x
                link(g, out_x)
                dve.wait_ge(*ln_rs[i](g, 6))
                return tt(tiles(xn), tiles(x), bcast(r2, D), ALU.mult)

            def clip(g, i, src, bias):
                ts(um[:, i % 2, :], src, bias, SOFTPLUS_CAP, ALU.add, ALU.min).then_inc(um_ready.sem, 1)

            def scan_inputs(g):
                dve.wait_ge(*emb_landed(g, 16 * TILES))
                tt(hM[:, :], emb[:, :], C("pe"), ALU.add).then_inc(emb_used.sem, 1)
                dve.wait_ge(*emb_used(g, 1))
                layernorm(g, 0, hM[:, :], xcM[:, :], sqM[:, :], xlM[:, :], stM, xnM[:, :]).then_inc(xn_ready.sem, 1)
                link(g, tt(hM[:, :], hM[:, :], xlM[:, :], ALU.add))
                for d in range(2):
                    dve.wait_ge(*upre_ready(g, d + 1))
                    clip(g, d, ps[2 + d][:, :], C("bc", d, 1))
                for d in range(2):
                    dve.wait_ge(*sl_ready(g, d + 1))
                    stt(u[:, d, :], ps[2 + d][:, :], C("bc", d, 1), um[:, d, :], ALU.add, ALU.max
                        ).then_inc(u_ready.sem, 1)
                dve.wait_ge(*u_ready(g, 2))
                for d in range(2):
                    dve.wait_ge(*hi_ready(g, d + 1))
                    if d:
                        dve.wait_ge(*sx_ready(g, 1))
                    for j in range(2):
                        i = stt(r1[:, j * N:(j + 1) * N], hi[:, j * N:(j + 1) * N], C("n1", rows=96),
                                ps[2 * d + j][0:96, :], ALU.mult, ALU.add)
                    i.then_inc(r1_ready.sem, 1)
                    dve.wait_ge(*r1_ready(g, d + 1))
                    dve.wait_ge(*mid_ready(g, d + 1))
                    stt(SX[:, d, :], mid[:, :], C("n2", rows=96), r1, ALU.mult, ALU.add
                        ).then_inc(sx_ready.sem, 1)
                dve.wait_ge(*sx_ready(g, 2))
                for d in range(2):
                    dve.wait_ge(*dpre_ready(g, d + 1))
                    clip(g, 2 + d, ps[2 * d][:, :], C("bdt", d, 1))
                dve.wait_ge(*u_ready(g, 2))
                for d in range(2):
                    ts(acc[:, d, :], u[:, d, :], C("Dskip", d, 1), None, ALU.mult).then_inc(acc_init.sem, 1)
                for d in range(2):
                    dve.wait_ge(*sl_ready(g, 3 + d))
                    stt(delta[:, d, :], ps[2 * d][:, :], C("bdt", d, 1), um[:, d, :], ALU.add, ALU.max
                        ).then_inc(delta_ready.sem, 1)
                for d in range(2):
                    dve.wait_ge(*delta_ready(g, d + 1))
                    tt(du[:, d, :], delta[:, d, :], u[:, d, :], ALU.mult).then_inc(du_ready.sem, 1)

            def weigh_b(g, k):
                d = k // STATES
                dve.wait_ge(*b_ready(g, k + 1))
                dve.wait_ge(*du_ready(g, d + 1))
                tt(bx[:, k % 2, :], du[:, d, :], ps[k % 2][:, :], ALU.mult).then_inc(bx_done.sem, 1)

            def scan_states(g):
                weigh_b(g, 0)
                for k in range(2 * STATES):
                    d, turn = k // STATES, slice(None, None, -1 if k >= STATES else 1)
                    dve.wait_ge(*dA_ready(g, k + 1))
                    dve.wait_ge(*bx_done(g, k + 1))
                    dve.tensor_tensor_scan(hs[:, k % 2, turn], dA[:, d, k % RING, turn], bx[:, k % 2, turn], 0.0,
                                           ALU.mult, ALU.add).then_inc(h_done.sem, 1)
                    if k + 1 < 2 * STATES:
                        weigh_b(g, k + 1)
                    dve.wait_ge(*c_ready(g, k + 1))
                    dve.wait_ge(*h_done(g, k + 1))
                    if k >= RING:
                        dve.wait_ge(*acc_done(g, k - RING + 1))
                    tt(pC[:, k % RING, :], hs[:, k % 2, :], ps[2 + k % 2][:, :], ALU.mult).then_inc(p_done.sem, 1)
                dve.wait_ge(*acc_done(g, 2 * STATES))
                dve.wait_ge(*th_ready(g, 3))
                dve.wait_ge(*z1_ready(g, 1))
                stt(sy[:, 0, :], th[:, 0, :], 1.0, acc[:, 0, :], ALU.add, ALU.mult)
                link(g, stt(sy[:, 1, :], th[:, 1, :], 1.0, acc[:, 1, :], ALU.add, ALU.mult))
                stt(th[:, 2, :], th[:, 2, :], 1.0, z1[:, :], ALU.add, ALU.mult)
                link(g, tt(sy[:, 0, :], sy[:, 0, :], sy[:, 1, :], ALU.add))
                stt(mF, sy[:, 0, :], 0.25, th[:, 2, :], ALU.mult, ALU.mult).then_inc(m_ready.sem, 1)
                dve.wait_ge(*mT_ready(g, 1))
                tt(hB[:, :], hM[:, :], ps[0][:, :], ALU.add).then_inc(h1_ready.sem, 1)

            def route(g):
                e8 = EXPERTS

                def t3(j):
                    return rt[:, j, :].rearrange("p (k e) -> p k e", e=e8)

                mx, sm, ri, m1, i1, m2, i2, dn, rd = (rs8[:, j, :] for j in range(9))
                logits = rb[1][:, 0:TILES * e8].rearrange("p (k e) -> p k e", e=e8)
                iota = C("iota").rearrange("p (k e) -> p k e", e=e8)
                dve.wait_ge(*lg_ready(g, 1))
                link(g, red(mx, logits, AX.X, ALU.max))
                tt(t3(0), logits, bcast(mx, e8), ALU.subtract).then_inc(ls_ready.sem, 1)
                dve.wait_ge(*le_ready(g, 1))
                link(g, red(sm, t3(1), AX.X, ALU.add))
                link(g, dve.reciprocal(ri, sm))
                link(g, tt(t3(2), t3(1), bcast(ri, e8), ALU.mult))
                for m, i, onehot, rest in ((m1, i1, 4, 6), (m2, i2, 5, None)):
                    probs = t3(2) if rest else t3(6)
                    link(g, red(m, probs, AX.X, ALU.max))
                    link(g, tt(t3(3), probs, bcast(m, e8), ALU.is_equal))
                    link(g, stt(t3(3), t3(3), -float(e8), iota, ALU.mult, ALU.add))
                    link(g, red(i, t3(3), AX.X, ALU.min))
                    link(g, stt(t3(onehot), iota, -float(e8), bcast(i, e8), ALU.add, ALU.is_equal))
                    if rest:
                        link(g, stt(t3(rest), t3(onehot), -2.0, t3(2), ALU.mult, ALU.add))
                link(g, tt(dn, m1, m2, ALU.add))
                link(g, ts(dn, dn, 1e-12, None, ALU.max))
                link(g, dve.reciprocal(rd, dn))
                tt(t3(4), t3(4), bcast(m1, e8), ALU.mult)
                link(g, tt(t3(5), t3(5), bcast(m2, e8), ALU.mult))
                link(g, tt(t3(4), t3(4), t3(5), ALU.add))
                tt(comb[:, :].rearrange("p (k e) -> p k e", e=e8), t3(4), bcast(rd, e8), ALU.mult
                   ).then_inc(comb_ready.sem, 1)
                dve.wait_ge(*cTp_ready(g, 1))
                dve.tensor_copy(cT[:, :], rb[2][0:16, :]).then_inc(cT_ready.sem, 1)

            def experts(g):
                dve.wait_ge(*h1_ready(g, 1))
                link(g, dve.tensor_copy(hR[:, :], hB[:, :]))
                layernorm(g, 1, hR[:, :], xcR[:, :], sqR[:, :], xR[:, :], stR).then_inc(xm_ready.sem, 1)
                dve.wait_ge(*xm_ready(g, 1))
                link(g, tt(hR[:, :], hR[:, :], xR[:, :], ALU.add))
                route(g)
                for v in range(8):
                    dve.wait_ge(*ge_ready(g, v + 1))
                    dve.wait_ge(*cb_ready(g, v + 1))
                    if v >= 2:
                        dve.wait_ge(*mo_mm(g, v - 1))
                    tt(gg[:, v % 2, :], ge[:, v % 2, :], rb[2], ALU.mult).then_inc(gg_ready.sem, 1)
                dve.wait_ge(*moT_ready(g, 1))
                link(g, tt(hR[:, :], hR[:, :], rb[0], ALU.add))

            def attention(g):
                s = layernorm(g, 2, hR[:, :], xcR[:, :], sqR[:, :], xR[:, :], stR)
                s.then_inc(xa_ready.sem, 1)
                dve.wait_ge(*xa_ready(g, 1))
                dve.wait_ge(*ln_rs[2](g, 6))
                tt(tiles(xnR[:, :]), tiles(xR[:, :]), bcast(stR[:, 5, :], D), ALU.mult).then_inc(xa_ready.sem, 1)
                link(g, tt(hR[:, :], hR[:, :], xR[:, :], ALU.add))
                for i in range(4):
                    dve.wait_ge(*pj_ready(g, 12 + i + 1))
                    dve.tensor_copy(vT[:, i, :], rb[i % RING]).then_inc(pjV_done.sem, 1)
                dve.wait_ge(*pjV_done(g, 4))

                def row_max(w):
                    dve.wait_ge(*sc_ready(g, w + 1))
                    red(nmx[:, w % 4, :], rb[w % RING].rearrange("p (c t) -> p c t", c=2), AX.X, ALU.max,
                        negate=True).then_inc(nmx_ready.sem, 1)

                def scale_v(w):
                    sb_, a, r = w // 8, w // 4 % 2, w % 4
                    s, b = divmod(sb_, 2)
                    h = 4 * b + r
                    dve.wait_ge(*exp_done(g, 2 * w + 2))
                    dve.reciprocal(rinv[:, w % 4, :], rsum[:, w % 4, :]).then_inc(rinv_ready.sem, 1)
                    if w >= RING:
                        dve.wait_ge(*ot_done(g, w - RING + 1))
                    dve.wait_ge(*rinv_ready(g, w + 1))
                    v = vT[:, 2 * s + a, :].rearrange("p (c m) -> p c m", c=2)[:, :, h * HEAD_DIM:(h + 1) * HEAD_DIM]
                    tt(vs[:, w % RING, :, :], v, bcast(rinv[:, w % 4, :], HEAD_DIM), ALU.mult
                       ).then_inc(vs_ready.sem, 1)

                for w in range(33):
                    if w < 32:
                        row_max(w)
                    if w >= 1:
                        scale_v(w - 1)
                    if w >= 8 and w % 8 == 0:
                        i = w // 8 - 1
                        dve.wait_ge(*ot_done(g, 8 * i + 8))
                        dve.wait_ge(*pjA_done(g, i + 1))
                        stt(og[:, i, :], thg[:, i, :], 1.0, rb[3], ALU.add, ALU.mult).then_inc(og_ready.sem, 1)
                dve.wait_ge(*foT_ready(g, 1))
                link(g, tt(hR[:, :], hR[:, :], rb[1], ALU.add))

            def binary(g):
                layernorm(g, 3, hR[:, :], xcR[:, :], sqR[:, :], xR[:, :], stR).then_inc(xf_ready.sem, 1)
                dve.wait_ge(*gp_ready(g, 1))
                ts(G[:, :], rb[1][0:96, :], C("pb", rows=96), 0.0, ALU.add, ALU.is_gt).then_inc(G_ready.sem, 1)
                dve.wait_ge(*xfF_ready(g, 2))
                for w in range(D):
                    dve.wait_ge(*sg_ready(g, w + 1))
                    if w >= RING:
                        dve.wait_ge(*red_done(g, w - RING + 1))
                    tt(zz[:, w % RING, :], sg[:, w % RING, :], xb[:, :], ALU.mult).then_inc(zz_ready.sem, 1)
                dve.wait_ge(*yT_ready(g, 1))
                dve.wait_ge(*stored(g, 0))
                tt(outT[:, :], hR[:, :], rb[0], ALU.add).then_inc(out_ready.sem, 1)

            dve.wait_ge(loaded.sem, 16 * LOADS)
            dve.memset(dA[:, :, :, :], 0.0).then_inc(prepared.sem, 1)
            ts(half_bg[:, :], C("bg"), 0.5, None, ALU.mult).then_inc(prepared.sem, 1)
            ts(half_Wf[:, :, :].rearrange("p b d -> p (b d)"), C("Wf"), 0.5, None, ALU.mult).then_inc(prepared.sem, 1)
            dve.wait_ge(prepared.sem, 3 + 1 + 1)
            ts(negA[:, :], negA[:, :], -1.0, None, ALU.mult).then_inc(prepared.sem, 1)
            for d in range(2):
                dve.tensor_copy(Wdt[:, d, :], ps[d][:, 0:P]).then_inc(prepared.sem, 1)
            n = 3 + 1 + 1 + 3
            for q in range(8):
                w = kz[0:96, q, :]
                dve.tensor_copy(zz[0:96, 0, :], w).then_inc(prepared.sem, 1)
                dve.wait_ge(prepared.sem, n + 1)
                stt(w, zz[0:96, 0, :], C("w_n1", rows=96), w, ALU.mult, ALU.add).then_inc(prepared.sem, 1)
                dve.wait_ge(prepared.sem, n + 2)
                dve.tensor_copy(zz[0:96, 1, :], w).then_inc(prepared.sem, 1)
                dve.wait_ge(prepared.sem, n + 3)
                stt(w, zz[0:96, 1, :], C("w_n2", rows=96), w, ALU.mult, ALU.add).then_inc(prepared.sem, 1)
                dve.wait_ge(prepared.sem, n + 4)
                n += 4
                for s in range(2):
                    ts(Wt[:, 8 * q:8 * q + 8, s * D:(s + 1) * D], w.rearrange("p (o i) -> p o i", i=D),
                       C("w_s", s, 1, 96), None, ALU.mult).then_inc(prepared.sem, 1)
                n += 2
            dve.wait_ge(prepared.sem, n)
            dve.memset(kz[:, :, :], 0.0).then_inc(prepared.sem, 1)
            assert n + 1 == PREPARED, n
            with dve.Fori(0, GROUPS) as g:
                scan_inputs(g)
                scan_states(g)
                experts(g)
                attention(g)
                binary(g)
            assert step[0] == V_CHAIN, step[0]


def layout(inputs):
    import numpy as np

    f = np.float32
    c = np.zeros((P, NCONST), f)

    def at(name, i=0, w=None):
        a, width = COL[name]
        w = width if w is None else w
        return c[:, a + i * w:a + (i + 1) * w]

    L0 = {k[len("L0_attn_"):]: np.asarray(v) for k, v in inputs.items() if k.startswith("L0_attn_")}
    E0 = {k[len("L0_ffn_"):]: np.asarray(v) for k, v in inputs.items() if k.startswith("L0_ffn_")}
    L1 = {k[len("L1_attn_"):]: np.asarray(v) for k, v in inputs.items() if k.startswith("L1_attn_")}
    E1 = {k[len("L1_ffn_"):]: np.asarray(v) for k, v in inputs.items() if k.startswith("L1_ffn_")}
    at("ident")[:] = np.eye(P)
    for s in range(2):
        r = slice(s * D, s * D + D)
        at("Wp")[r, r] = L0["Wp"]
        for d, x in enumerate("fb"):
            at("Wc", d, 128)[r, r] = L0["Wc" + x].T
            for j in range(2):
                for part in range(3):
                    k = part * 32 + s * 16
                    at("Wx", 2 * d + j, 96)[r, k:k + 16] = L0["Wdbc_" + x][:, 16 + 16 * j:32 + 16 * j]
            rr = slice(s * 16, s * 16 + 16)
            at("dt_in" if d == 0 else "dt_in_b")[rr, r] = L0["Wdbc_" + x][:, :16].T
            at("dt_out", d, 128)[rr, r] = L0["Wdt_" + x]
            at("bc")[r, d] = L0["bc" + x]
            at("bdt")[r, d] = L0["bdt_" + x]
            at("Dskip")[r, d] = L0["D_" + x]
            at("Alog", d, 16)[r] = L0["Alog_" + x]
        for name, v in (("ln_g", L0["ln_g"]), ("ln_b", L0["ln_b"]), ("bp", L0["bp"]), ("gamma", L1["ln_gamma"]),
                        ("beta", L1["ln_beta"]), ("bf", L1["b_final"])):
            at(name)[r, 0] = v
        for ep in range(4):
            for e in range(2):
                at("W1", 2 * ep + s, 128)[r, e * D:(e + 1) * D] = E0["w1"][2 * ep + e]
        at("b2")[s * 8:s * 8 + 8, r] = E0["b2"]
        at("router")[r, s * 8:s * 8 + 8] = E0["router_w"].T
        for b in range(2):
            m = slice(b * P, b * P + P)
            at("Wq", 2 * s + b, 128)[r] = L1["W_qkv"][m].T
            at("Wk", 2 * s + b, 128)[r] = L1["W_qkv"][256:][m].T
            at("Wg", 2 * s + b, 128)[r] = L1["W_gate"][m].T
        at("Wv", s, 256)[r] = L1["W_qkv"][512:].T
        for part in range(3):
            k = part * 16 + s * 8
            at("proj")[r, k:k + 8] = E1["proj_w"].T
            at("pb")[k:k + 8, 0] = E1["proj_b"]
            at("w_s")[k:k + 8, s] = 1
        for q in range(4):
            k = q * 32 + s * 16
            at("scale")[k:k + 16, 0] = E1["scale"][0, 0, q * 16:(q + 1) * 16]
            for o in range(16):
                at("perm")[k + o, s * D + q * 16 + o] = 1
    at("pb")[48:96] = -1
    for ep in range(4):
        for e in range(2):
            at("W2", ep, 64)[e * D:(e + 1) * D] = E0["w2"][2 * ep + e]
            at("b1")[e * D:(e + 1) * D, ep] = E0["b1"][2 * ep + e]
    for b in range(2):
        at("bg")[:, b] = L1["b_gate"][b * P:(b + 1) * P]
        at("Wf", b, 64)[:] = L1["W_final"][:, b * P:(b + 1) * P].T
    at("n1")[32:96] = -1
    at("n2")[64:96] = -1
    at("w_n1")[16:48] = -1
    at("w_n2")[32:48] = -1
    at("mhalf")[:] = -0.5
    at("eps64")[:] = D * EPS
    at("eps")[:] = EPS
    at("iota")[:] = np.tile(np.arange(EXPERTS, dtype=f), TILES)
    pos = np.arange(SEQ, dtype=f)[:, None]
    dim = np.arange(D)
    inv = np.power(f(10000.0), -((dim - dim % 2).astype(f) / f(D)), dtype=f)
    angle = (pos * inv).astype(f)
    pe = np.where(dim % 2 == 0, np.sin(angle), np.cos(angle)).astype(f)
    at("pe").reshape(P, 2, 2, 2, D)[:] = pe.reshape(2, P, D).transpose(1, 0, 2)[:, None, :, None, :]

    one = 0x3F80
    sel = np.zeros((96, STATES, P), np.uint16)
    for part in range(3):
        for s in range(2):
            for n in range(STATES):
                sel[part * 32 + s * 16 + n, n, s * D:(s + 1) * D] = one
    ones = np.zeros((P, 16, 32), np.uint16)
    for s in range(2):
        for j in range(16):
            ones[s * D:(s + 1) * D, j, s * 16 + j] = one
    w = np.zeros((96, 8, N), f)
    wt = E1["weight"][0].transpose(0, 2, 1).reshape(EXPERTS, 8, N)
    for k in range(6):
        w[k * 8:k * 8 + 8] = wt
    x = np.asarray(inputs["x"]).astype(np.int32)
    ids = np.zeros((P, (GROUPS + 1) * TILES), np.int32)
    ids[:, :GROUPS * TILES] = x.reshape(GROUPS, 2, 2, 2, P).transpose(4, 0, 1, 3, 2).reshape(P, -1)
    return {"table": np.ascontiguousarray(inputs["L0_tok_W"]), "ids": ids, "consts": c, "selectors": sel,
            "ones_sel": ones, "w_exp": w}


def kernel(**inputs):
    import numpy as np
    from concourse import bacc
    from concourse.bass_utils import run_bass_kernel_spmd

    nc = bacc.Bacc("TRN2", target_bir_lowering=False, num_devices=1)
    arrays = layout(inputs)
    args = [nc.dram_tensor(k, a.shape, mybir.dt.from_np(a.dtype), kind="ExternalInput").ap()
            for k, a in arrays.items()]
    args.append(nc.dram_tensor("out", (GROUPS * P, N), F32, kind="ExternalOutput").ap())
    build_tower(nc, *args)
    r = run_bass_kernel_spmd(nc, [arrays], core_ids=[0])
    got = np.asarray(r.results[0]["out"]).reshape(GROUPS, P, 2, 2, 2, D)
    return got.transpose(0, 2, 4, 3, 1, 5).reshape(BATCH, SEQ, D)
```

```python
from contextlib import ExitStack

import concourse.bass as bass
from concourse import mybir

F32 = mybir.dt.float32
BF16 = mybir.dt.bfloat16
I32 = mybir.dt.int32
U16 = mybir.dt.uint16
ALU = mybir.AluOpType
ACT = mybir.ActivationFunctionType
AX = mybir.AxisListType

P = 128
D = 64
SEQ = 256
BATCH = 32
GROUPS = 8
N = 512
TILES = 8
STATES = 16
DT_RANK = 16
EXPERTS = 8
HEADS = 8
HEAD_DIM = 32
EPS = 1e-5
STATE0, STATE_DT = 44, 2.5
ATT0, ATT_DT = 2, 1.7
ATT1 = ATT0 + ATT_DT * 34
BIN0, BIN_DT = ATT1 + 8, 0.7
PREP0 = 58
TAIL0 = 126
END = BIN0 + 15 + BIN_DT * (D + 2) + 1
SOFTPLUS_CAP = 40.0
RING = 3

_WIDTHS = [
    ("ident", 128), ("perm", 128), ("Wp", 128), ("Wc", 256), ("Wx", 4 * 96), ("dt_in", 128), ("dt_out", 256),
    ("dt_in_b", 128), ("W1", 8 * 128), ("W2", 4 * 64), ("b2", 128), ("router", 16), ("Wq", 512), ("Wk", 512),
    ("Wv", 512), ("Wg", 512), ("Wf", 128), ("proj", 96), ("pe", 512), ("iota", 64), ("mhalf", 8), ("eps64", 8), ("eps", 8),
    ("ln_g", 1), ("ln_b", 1), ("bp", 1), ("bc", 2), ("bdt", 2), ("Dskip", 2), ("Alog", 32), ("b1", 4),
    ("gamma", 1), ("beta", 1), ("bg", 2), ("bf", 1), ("scale", 1), ("pb", 1), ("n1", 1), ("n2", 1),
    ("w_n1", 1), ("w_n2", 1), ("w_s", 2),
]
COL, _at = {}, 0
for _name, _w in _WIDTHS:
    COL[_name] = (_at, _w)
    _at += _w
NCONST = _at


class Signal:

    def __init__(self, sem, per, seed=0):
        self.sem, self.per, self.seed = sem, per, seed

    def __call__(self, g, k):
        return self.sem, g * self.per + (k + self.seed)


def weave(*stages):
    at = [(next(s), i) for i, s in enumerate(stages)]
    while at:
        slot, i = min(at)
        at.remove((slot, i))
        following = next(stages[i], None)
        if following is not None:
            at.append((max(following, slot), i))


def iterations(fori, scan, experts, attention):
    weave(scan(0))
    weave(scan(1), experts(0))
    with fori(2, GROUPS) as i:
        weave(scan(i), experts(i - 1), attention(i - 2))
    weave(experts(GROUPS - 1), attention(GROUPS - 2))
    weave(attention(GROUPS - 1))


def not_first(g):
    return not isinstance(g, int) or g > 0


def bcast(ap, n):
    p, m = ap.shape
    return ap.unsqueeze(2).to_broadcast([p, m, n])


def build_tower(nc, table, ids, consts, selectors, ones_sel, w_exp, out):
    with ExitStack() as ctx:
        def sb(name, shape, dt=F32):
            return ctx.enter_context(nc.sbuf_tensor(name, shape, dt))

        signals = {}

        def sig(name, per, seed=0):
            s = Signal(ctx.enter_context(nc.semaphore(name)), per, seed)
            signals[name] = s
            return s

        cst = sb("cst", [P, NCONST])

        def C(name, i=0, w=None, rows=P):
            at, width = COL[name]
            w = width if w is None else w
            return cst[0:rows, at + i * w:at + (i + 1) * w]

        ident = C("ident")
        sel = sb("sel", [96, STATES, P], BF16)
        ones_w = sb("ones_w", [P, 16, 32], BF16)
        Wt = sb("Wt", [96, D, P], BF16)
        idx_all = sb("idx_all", [P, (GROUPS + 1) * TILES], I32)
        idx = sb("idx", [P, TILES], I32)
        negA = sb("negA", [P, 2 * STATES])
        Wdt = sb("Wdt", [P, 2, P])
        half_bg = sb("half_bg", [P, 2])
        half_Wf = sb("half_Wf", [P, 2, D])

        emb = sb("emb", [P, N])
        hM = sb("hM", [P, N])
        hB = sb("hB", [P, N])
        xcM, sqM = sb("xcM", [P, N]), sb("sqM", [P, N])
        xlM, xnM = sqM, xcM
        stM = sb("stM", [P, 8, TILES])
        z1 = sb("z1", [P, N])
        um = sb("um", [P, 2, N])
        u = sb("u", [P, 2, N])
        r1 = um[0:96, :, :].rearrange("p j n -> p (j n)")
        SX = sb("SX", [96, 2, 2 * N], BF16)
        delta = sb("delta", [P, 2, N])
        du = sb("du", [P, 2, N])
        dA = sb("dA", [P, 2, RING, N])
        bx = sb("bx", [P, 2, N])
        hs = sb("hs", [P, 2, N])
        hi, mid = (bx[0:96, j, :].bitcast(BF16) for j in range(2))
        pC = sb("pC", [P, RING, N])
        xnF = pC[:, 0, :]
        acc = sb("acc", [P, 2, N])
        th, sy, mF = pC, bx, hs[:, 0, :]

        hR = sb("hR", [P, N])
        xcR, sqR = sb("xcR", [P, N]), sb("sqR", [P, N])
        xR, xnR = sqR, xcR
        stR = sb("stR", [P, 8, TILES])
        aF = sb("aF", [P, N])
        nF = sb("nF", [P, N])
        rt = sb("rt", [P, 7, TILES * EXPERTS])
        rs8 = sb("rs8", [P, 9, TILES])
        comb = sb("comb", [P, TILES * EXPERTS])
        cT = nF[0:16, :]
        ge = sb("ge", [P, 4, N])
        qF = sb("qF", [P, 4, N])
        kF = ge
        kz = sb("kz", [P, 16, N])
        vT = sb("vT", [P, 4, N])
        thg = sb("thg", [P, 4, N])
        og = thg

        hS = sb("hS", [P, N])
        xcS, sqS = sb("xcS", [P, N]), sb("sqS", [P, N])
        xS = sqS
        stS = sb("stS", [P, 8, TILES])
        aS = sb("aS", [P, N])
        nmx = sb("nmx", [P, 4, 2])
        rsum = sb("rsum", [P, 4, 2])
        rinv = sb("rinv", [P, 4, 2])
        prob = sb("prob", [P, RING, 2, SEQ])
        vs = sb("vs", [P, RING, 2, HEAD_DIM])
        xb = sb("xb", [P, N], BF16)
        G = sb("G", [96, N], BF16)
        sg = sb("sg", [P, RING, N], BF16)
        outT = hS

        banks = [ctx.enter_context(nc.psum_tensor(f"ps{i}", [P, N], F32)) for i in range(8)]
        mb, eb, bb = ([b[:, :] for b in x] for x in (banks[0:2], banks[2:5], banks[5:8]))

        loaded = sig("loaded", 0)
        prepared = sig("prepared", 0)
        emb_landed = sig("emb_landed", 16 * TILES)
        idx_copied = sig("idx_copied", 1)
        emb_used = sig("emb_used", 1)
        chain_m, chain_e, chain_s = sig("chain_m", 5), sig("chain_e", 25), sig("chain_s", 2)
        ln_xc = [sig(f"ln_xc{i}", 1) for i in range(4)]
        ln_sq = [sig(f"ln_sq{i}", 1) for i in range(4)]
        ln_var = [sig(f"ln_var{i}", 1) for i in range(4)]
        ln_rs = [sig(f"ln_rs{i}", 6 if i in (0, 2) else 2) for i in range(4)]
        xn_ready = sig("xn_ready", 1)
        xnT_ready = sig("xnT_ready", 1)
        xnF_ready = sig("xnF_ready", 1)
        z1p_ready = sig("z1p_ready", 1)
        z1_ready = sig("z1_ready", 1)
        upre_ready = sig("upre_ready", 2)
        lin_ready = sig("lin_ready", 4)
        um_ready = sig("um_ready", 4)
        se_ready = sig("se_ready", 4)
        sl_ready = sig("sl_ready", 4)
        u_ready = sig("u_ready", 2)
        xp_ready = sig("xp_ready", 2)
        hi_ready = sig("hi_ready", 2)
        r1_ready = sig("r1_ready", 2)
        mid_ready = sig("mid_ready", 2)
        sx_ready = sig("sx_ready", 2)
        dpre_ready = sig("dpre_ready", 2)
        delta_ready = sig("delta_ready", 2)
        du_ready = sig("du_ready", 2)
        acc_init = sig("acc_init", 2)
        b_ready = sig("b_ready", 2 * STATES)
        c_ready = sig("c_ready", 2 * STATES)
        dA_ready = sig("dA_ready", 2 * STATES)
        bx_done = sig("bx_done", 2 * STATES)
        h_done = sig("h_done", 2 * STATES)
        p_done = sig("p_done", 2 * STATES)
        acc_done = sig("acc_done", 2 * STATES)
        th_ready = sig("th_ready", 3)
        m_ready = sig("m_ready", 1)
        mT_ready = sig("mT_ready", 1)
        h1_ready = sig("h1_ready", 1)

        xm_ready = sig("xm_ready", 1)
        xmT_ready = sig("xmT_ready", 1)
        xmF_ready = sig("xmF_ready", 1)
        lg_ready = sig("lg_ready", 1)
        ls_ready = sig("ls_ready", 1)
        le_ready = sig("le_ready", 1)
        comb_ready = sig("comb_ready", 1)
        cTp_ready = sig("cTp_ready", 1)
        cT_ready = sig("cT_ready", 1)
        hp_ready = sig("hp_ready", 8)
        cb_ready = sig("cb_ready", 8)
        ge_ready = sig("ge_ready", 8)
        gg_ready = sig("gg_ready", 8)
        mo_mm = sig("mo_mm", 8)
        moF_ready = sig("moF_ready", 1)
        moT_ready = sig("moT_ready", 1)
        xa_ready = sig("xa_ready", 2)
        xaT_ready = sig("xaT_ready", 2)
        xaF_ready = sig("xaF_ready", 2)
        pj_ready = sig("pj_ready", 16)
        pjA_done = sig("pjA_done", 12)
        pjV_done = sig("pjV_done", 4)
        kz_landed = sig("kz_landed", 16 * 16)
        sc_ready = sig("sc_ready", 32)
        nmx_ready = sig("nmx_ready", 32)
        exp_done = sig("exp_done", 64)
        rinv_ready = sig("rinv_ready", 32)
        vs_ready = sig("vs_ready", 32)
        ot_done = sig("ot_done", 32)
        og_ready = sig("og_ready", 4)
        fo_ready = sig("fo_ready", 1)
        foF_ready = sig("foF_ready", 1)
        foT_ready = sig("foT_ready", 1)
        xf_ready = sig("xf_ready", 1)
        xfT_ready = sig("xfT_ready", 1)
        xfF_ready = sig("xfF_ready", 2)
        gp_ready = sig("gp_ready", 1)
        G_ready = sig("G_ready", 1)
        w_ready = sig("w_ready", D)
        sg_ready = sig("sg_ready", D)
        zz_ready = sig("zz_ready", D)
        red_done = sig("red_done", D)
        yF_ready = sig("yF_ready", 1)
        yT_ready = sig("yT_ready", 1)
        hS_ready = sig("hS_ready", 1)
        hR_done = sig("hR_done", 1)
        out_ready = sig("out_ready", 1)
        stored = sig("stored", 16, seed=16)

        LOADS = 5
        PREP_V = 3 + 3 + 8 * 6 + 1
        PREPARED = 1 + 1 + PREP_V

        block = ctx.enter_context(nc.Block())

        @block.sync
        def _(sp):
            sp.dma_start(idx_all[:, :], ids).then_inc(loaded.sem, 16)
            sp.dma_start(cst[:, :], consts).then_inc(loaded.sem, 16)
            sp.dma_start(sel[:, :, :].bitcast(U16), selectors).then_inc(loaded.sem, 16)
            sp.dma_start(ones_w[:, :, :].bitcast(U16), ones_sel).then_inc(loaded.sem, 16)
            sp.dma_start(kz[0:96, 0:8, :], w_exp).then_inc(loaded.sem, 16)
            sp.sem_inc(stored.sem, 16)

            def scan(g):
                yield 0

            def experts(g):
                yield 80
                for i in range(4):
                    sp.wait_ge(*pjA_done(g, 4 + i + 1))
                    if not_first(g):
                        sp.wait_ge(*sc_ready(g - 1, 32))
                    for r in range(4):
                        rows = slice(32 * r, 32 * r + 32)
                        sp.dma_start(kz[rows, 4 * i + r, :], kF[rows, i, :]).then_inc(kz_landed.sem, 16)

            def attention(g):
                yield END + 3
                sp.wait_ge(*out_ready(g, 1))
                start = g * P
                sp.dma_start(out[bass.ds(start, P), :], outT[:, :]).then_inc(stored.sem, 16)

            iterations(sp.Fori, scan, experts, attention)
            sp.wait_ge(*stored(GROUPS, 0))
            sp.wait_ge(*emb_landed(GROUPS + 1, 0))

        @block.gpsimd
        def _(pool):
            def gather(k):
                pool.indirect_dma_start(emb[:, k * D:(k + 1) * D], None, table,
                                        bass.IndirectOffsetOnAxis(ap=idx[:, k:k + 1], axis=0)
                                        ).then_inc(emb_landed.sem, 16)

            def root(g, i, st):
                var, rs, t, v2, r2 = (st[:, j, :] for j in range(1, 6))
                done = ln_rs[i]
                pool.wait_ge(*ln_var[i](g, 1))
                pool.tensor_tensor(t, var, C("eps64"), ALU.add).then_inc(done.sem, 1)
                pool.wait_ge(*done(g, 1))
                pool.tensor_tensor(rs, t, C("mhalf"), ALU.pow).then_inc(done.sem, 1)
                if done.per == 6:
                    pool.wait_ge(*done(g, 2))
                    pool.tensor_tensor(t, rs, rs, ALU.mult).then_inc(done.sem, 1)
                    pool.wait_ge(*done(g, 3))
                    pool.tensor_tensor(v2, t, var, ALU.mult).then_inc(done.sem, 1)
                    pool.wait_ge(*done(g, 4))
                    pool.tensor_tensor(v2, v2, C("eps"), ALU.add).then_inc(done.sem, 1)
                    pool.wait_ge(*done(g, 5))
                    pool.tensor_tensor(r2, v2, C("mhalf"), ALU.pow).then_inc(done.sem, 1)

            pool.wait_ge(loaded.sem, 16 * LOADS)
            pool.tensor_copy(idx[:, :], idx_all[:, 0:TILES]).then_inc(idx_copied.sem, 1)
            pool.wait_ge(idx_copied.sem, 1)
            for k in range(TILES):
                gather(k)

            def scan(g):
                yield 0
                pool.wait_ge(*emb_landed(g, 16 * TILES))
                pool.wait_ge(*emb_used(g, 1))
                pool.tensor_copy(idx[:, :], idx_all[:, bass.ds(g * TILES + TILES, TILES)]).then_inc(idx_copied.sem, 1)
                yield 4.5
                pool.wait_ge(*idx_copied(g, 2))
                root(g, 0, stM)
                for k in range(TILES):
                    yield 14 + 3 * k
                    gather(k)
                for d in range(2):
                    for n in range(STATES):
                        k = d * STATES + n
                        yield STATE0 + STATE_DT * k + 2.5
                        if n == 0:
                            pool.wait_ge(*acc_init(g, d + 1))
                        pool.wait_ge(*p_done(g, k + 1))
                        if n:
                            pool.wait_ge(*acc_done(g, k))
                        pool.tensor_tensor(acc[:, d, :], acc[:, d, :], pC[:, k % RING, :], ALU.add
                                           ).then_inc(acc_done.sem, 1)

            def experts(g):
                yield 4.5
                root(g, 1, stR)
                yield PREP0 + 4
                root(g, 2, stR)

            def attention(g):
                yield BIN0 + 4
                root(g, 3, stS)

            iterations(pool.Fori, scan, experts, attention)

        @block.tensor
        def _(pe):
            def flip(dst, src):
                for k in range(4):
                    i = pe.transpose(dst[:, k * P:(k + 1) * P], src[:, k * P:(k + 1) * P], ident)
                return i

            def mm(dst, lhsT, rhs, start=True, stop=True):
                return pe.matmul(dst, lhsT, rhs, start=start, stop=stop)

            def scan(g):
                yield 13.5
                pe.wait_ge(*xn_ready(g, 1))
                flip(mb[0], xnM[:, :]).then_inc(xnT_ready.sem, 1)
                yield 16.5
                pe.wait_ge(*xnF_ready(g, 1))
                mm(mb[1], C("Wp"), xnF).then_inc(z1p_ready.sem, 1)
                for d in range(2):
                    yield 19 + d
                    if d == 0:
                        pe.wait_ge(*z1_ready(g, 1))
                    mm(mb[d], C("Wc", d, 128), z1[:, :]).then_inc(upre_ready.sem, 1)
                for d in range(2):
                    yield 27 + 5 * d
                    if d:
                        pe.wait_ge(*r1_ready(g, 1))
                    else:
                        pe.wait_ge(*u_ready(g, 2))
                    for j in range(2):
                        i = mm(mb[j][0:96, :], C("Wx", 2 * d + j, 96), u[:, d, :])
                    i.then_inc(xp_ready.sem, 1)
                for d in range(2):
                    yield 36.5 + d
                    pe.wait_ge(*r1_ready(g, 2))
                    mm(mb[d], Wdt[:, d, :], u[:, d, :]).then_inc(dpre_ready.sem, 1)
                for k in range(2 * STATES):
                    d, n = divmod(k, STATES)
                    yield STATE0 + STATE_DT * k - (1.7 if k else 1)
                    if k == 0:
                        pe.wait_ge(*delta_ready(g, 2))
                    else:
                        pe.wait_ge(*bx_done(g, k))
                    if n == 0:
                        pe.wait_ge(*sx_ready(g, d + 1))
                    mm(mb[0], sel[:, n, :], SX[:, d, 0:N]).then_inc(b_ready.sem, 1)
                    yield STATE0 + STATE_DT * k
                    if k:
                        pe.wait_ge(*p_done(g, k))
                    mm(mb[1], sel[:, n, :], SX[:, d, N:2 * N]).then_inc(c_ready.sem, 1)
                yield TAIL0 + 3
                pe.wait_ge(*m_ready(g, 1))
                flip(mb[0], mF).then_inc(mT_ready.sem, 1)

            def experts(g):
                def hidden(v):
                    if v % 4 >= 2:
                        pe.wait_ge(*ge_ready(g, v - 1))
                    mm(eb[v % 2], C("W1", v, 128), aF[:, :]).then_inc(hp_ready.sem, 1)

                def spread(v):
                    ep, s = divmod(v, 2)
                    if v % 4 >= 2:
                        pe.wait_ge(*gg_ready(g, v - 1))
                    for k in range(4):
                        for e in range(2):
                            at = k * 16 + s * 8 + ep * 2 + e
                            i = mm(eb[1 - v % 2][64 * e:64 * e + 64, k * P:(k + 1) * P],
                                   comb[:, at:at + 1].to_broadcast([P, 64]), ident)
                    i.then_inc(cb_ready.sem, 1)

                def expert_out(v):
                    ep, s = divmod(v, 2)
                    pe.wait_ge(*gg_ready(g, v + 1))
                    mm(eb[2][64 * s:64 * s + 64, :], C("W2", ep, 64), ge[:, v % 4, :], False, ep == 3
                       ).then_inc(mo_mm.sem, 1)

                yield 9
                pe.wait_ge(*xm_ready(g, 1))
                flip(eb[0], xR[:, :]).then_inc(xmT_ready.sem, 1)
                yield 12
                pe.wait_ge(*xmF_ready(g, 1))
                for k in range(4):
                    i = mm(eb[2][:, k * 16:(k + 1) * 16], aF[:, k * P:(k + 1) * P], C("router"))
                i.then_inc(lg_ready.sem, 1)
                yield 14
                for v in range(4):
                    hidden(v)
                yield 27
                pe.wait_ge(*comb_ready(g, 1))
                pe.wait_ge(*ge_ready(g, 4))
                for k in range(4):
                    i = mm(eb[0][0:16, k * P:(k + 1) * P], comb[:, k * 16:(k + 1) * 16], ident)
                i.then_inc(cTp_ready.sem, 1)
                spread(0)
                yield 29
                pe.wait_ge(*cT_ready(g, 1))
                for s in range(2):
                    mm(eb[2][64 * s:64 * s + 64, :], C("b2", s, 64, 16), cT, True, False)
                spread(1)
                for v in range(2, 4):
                    yield 31 + 2.5 * (v - 2)
                    spread(v)
                    expert_out(v - 2)
                yield 36
                expert_out(2)
                expert_out(3)
                yield 38
                for v in range(4, 8):
                    hidden(v)
                yield 43
                pe.wait_ge(*ge_ready(g, 8))
                spread(4)
                spread(5)
                for v in range(6, 8):
                    yield 46 + 2.5 * (v - 6)
                    spread(v)
                    expert_out(v - 2)
                yield 51
                expert_out(6)
                expert_out(7)
                yield 54
                pe.wait_ge(*moF_ready(g, 1))
                flip(eb[0], aF[:, :]).then_inc(moT_ready.sem, 1)
                yield PREP0 + 8
                pe.wait_ge(*xa_ready(g, 1))
                flip(eb[0], xR[:, :]).then_inc(xaT_ready.sem, 1)
                yield PREP0 + 13
                pe.wait_ge(*xa_ready(g, 2))
                flip(eb[1], xnR[:, :]).then_inc(xaT_ready.sem, 1)
                for w in range(16):
                    kind, i = divmod(w, 4)
                    yield (PREP0 + 17 if w < 12 else PREP0 + 23) + 1.3 * w
                    if w == 0:
                        pe.wait_ge(*xaF_ready(g, 2))
                    if w >= RING:
                        if w - RING < 8:
                            pe.wait_ge(*pjA_done(g, w - RING + 1))
                        elif w - RING < 12:
                            pe.wait_ge(*pjV_done(g, w - RING - 7))
                        else:
                            pe.wait_ge(*pjA_done(g, w - RING - 3))
                    bank = eb[w % RING]
                    if kind != 2:
                        m = mm(bank, C({0: "Wq", 1: "Wk", 3: "Wg"}[kind], i, 128), (aF if kind == 3 else nF)[:, :])
                    else:
                        s, a = divmod(i, 2)
                        for c in range(2):
                            at = (2 * a + c) * P
                            m = mm(bank[:, c * SEQ:(c + 1) * SEQ], nF[:, at:at + P], C("Wv", s, SEQ))
                    m.then_inc(pj_ready.sem, 1)

            def attention(g):
                def scores(w):
                    sb_, a, r = w // 8, w // 4 % 2, w % 4
                    if w >= 2:
                        pe.wait_ge(*exp_done(g, 2 * (w - 1)))
                    for c in range(2):
                        at = a * SEQ + c * P
                        m = mm(bb[w % 2][:, c * SEQ:(c + 1) * SEQ], qF[:, sb_, at:at + P],
                               kz[:, 4 * sb_ + r, a * SEQ:(a + 1) * SEQ])
                    m.then_inc(sc_ready.sem, 1)

                def weighted(w):
                    sb_, a, r = w // 8, w // 4 % 2, w % 4
                    if w % 8 == 0 and sb_:
                        pe.wait_ge(*og_ready(g, sb_))
                    pe.wait_ge(*vs_ready(g, w + 1))
                    for c in range(2):
                        m = mm(bb[2][32 * r:32 * r + 32, a * SEQ:(a + 1) * SEQ], vs[:, w % RING, c, :],
                               prob[:, w % RING, c, :], c == 0, c == 1)
                    m.then_inc(ot_done.sem, 1)

                for w in range(34):
                    yield ATT0 + ATT_DT * w
                    if w == 0:
                        pe.wait_ge(*kz_landed(g, 256))
                        pe.wait_ge(*pjA_done(g, 12))
                        if not_first(g):
                            pe.wait_ge(*out_ready(g - 1, 1))
                    if w < 32:
                        scores(w)
                    if w >= 2:
                        weighted(w - 2)
                yield ATT1 + 2
                for i in range(4):
                    s, b = divmod(i, 2)
                    pe.wait_ge(*og_ready(g, i + 1))
                    m = mm(bb[0][64 * s:64 * s + 64, :], half_Wf[:, b, :], og[:, i, :], b == 0, b == 1)
                m.then_inc(fo_ready.sem, 1)
                yield ATT1 + 6
                pe.wait_ge(*foF_ready(g, 1))
                flip(bb[1], aS[:, :]).then_inc(foT_ready.sem, 1)
                yield BIN0 + 9
                pe.wait_ge(*xf_ready(g, 1))
                flip(bb[0], xS[:, :]).then_inc(xfT_ready.sem, 1)
                yield BIN0 + 12
                pe.wait_ge(*xfF_ready(g, 2))
                mm(bb[1][0:96, :], C("proj"), aS[:, :]).then_inc(gp_ready.sem, 1)

                def expand(w):
                    if w >= 2:
                        pe.wait_ge(*sg_ready(g, w - 1))
                    o = 16 * (w % 4) + w // 4
                    mm(bb[w % 2], Wt[:, o, :], G[:, :]).then_inc(w_ready.sem, 1)

                def reduce(w):
                    q, j = w % 4, w // 4
                    pe.wait_ge(*zz_ready(g, w + 1))
                    mm(bb[2][32 * q:32 * q + 32, :], ones_w[:, j, :], sg[:, w % RING, :], j == 0, j == 15
                       ).then_inc(red_done.sem, 1)

                for w in range(D + 2):
                    yield BIN0 + 15 + BIN_DT * w
                    if w == 0:
                        pe.wait_ge(*G_ready(g, 1))
                    if w < D:
                        expand(w)
                    if w >= 2:
                        reduce(w - 2)
                yield END + 1
                pe.wait_ge(*yF_ready(g, 1))
                for k in range(4):
                    i = mm(bb[0][:, k * P:(k + 1) * P], aS[:, k * P:(k + 1) * P], C("perm"))
                i.then_inc(yT_ready.sem, 1)

            pe.wait_ge(loaded.sem, 16 * LOADS)
            mm(mb[0][:, 0:P], C("dt_in", 0, 128, 32), C("dt_out", 0, 128, 32))
            mm(mb[1][:, 0:P], C("dt_in_b", 0, 128, 32), C("dt_out", 1, 128, 32)).then_inc(prepared.sem, 1)
            pe.wait_ge(prepared.sem, PREPARED)
            iterations(pe.Fori, scan, experts, attention)

        @block.scalar
        def _(act):
            def square(g, i, dst, src):
                act.wait_ge(*ln_xc[i](g, 1))
                act.activation(dst, src, ACT.Square).then_inc(ln_sq[i].sem, 1)

            def softplus_log(g, i):
                act.wait_ge(*um_ready(g, i + 1))
                act.activation(um[:, i % 2, :], um[:, i % 2, :], ACT.Exp).then_inc(se_ready.sem, 1)
                act.wait_ge(*se_ready(g, i + 1))
                act.activation(um[:, i % 2, :], um[:, i % 2, :], ACT.Ln, bias=1.0).then_inc(sl_ready.sem, 1)

            def scan(g):
                yield 0
                act.preload_act_table_set("natural_log_exp_and_others")
                yield 2.5
                square(g, 0, sqM[:, :], xcM[:, :])
                yield 15
                act.wait_ge(*xnT_ready(g, 1))
                act.activation(xnF, mb[0], ACT.Identity, bias=C("ln_b"), scale=C("ln_g")
                               ).then_inc(xnF_ready.sem, 1)
                yield 18
                act.wait_ge(*z1p_ready(g, 1))
                act.activation(z1[:, :], mb[1], ACT.Identity, bias=C("bp")).then_inc(z1_ready.sem, 1)
                for d in range(2):
                    yield 22.5 + 1.5 * d
                    softplus_log(g, d)
                for d in range(2):
                    yield 28.5 + 5 * d
                    act.wait_ge(*xp_ready(g, d + 1))
                    for j in range(2):
                        i = act.activation(hi[:, j * N:(j + 1) * N], mb[j][0:96, :], ACT.Copy)
                    i.then_inc(hi_ready.sem, 1)
                    yield 31.5 + 5 * d
                    act.wait_ge(*r1_ready(g, d + 1))
                    act.activation(mid, r1, ACT.Copy).then_inc(mid_ready.sem, 1)
                for d in range(2):
                    yield 39 + 1.5 * d
                    softplus_log(g, 2 + d)
                for k in range(2 * STATES):
                    d, n = divmod(k, STATES)
                    yield STATE0 + STATE_DT * k - 2
                    if n == 0:
                        act.wait_ge(*delta_ready(g, d + 1))
                    if n >= RING:
                        act.wait_ge(*h_done(g, k - RING + 1))
                    cols = slice(1, SEQ) if d == 0 else slice(0, SEQ - 1)
                    src = delta[:, d, :].rearrange("p (a t) -> p a t", a=2)[:, :, cols]
                    dst = dA[:, d, n % RING, :].rearrange("p (a t) -> p a t", a=2)[:, :, cols]
                    act.activation(dst, src, ACT.Exp, scale=negA[:, k:k + 1]).then_inc(dA_ready.sem, 1)
                yield TAIL0
                act.wait_ge(*acc_done(g, 2 * STATES))
                for d, src in enumerate((acc[:, 0, :], acc[:, 1, :], z1[:, :])):
                    act.activation(th[:, d, :], src, ACT.Tanh, scale=0.5).then_inc(th_ready.sem, 1)

            def experts(g):
                yield 2.5
                square(g, 1, sqR[:, :], xcR[:, :])
                yield 10.5
                act.wait_ge(*xmT_ready(g, 1))
                act.activation(aF[:, :], eb[0], ACT.Copy).then_inc(xmF_ready.sem, 1)

                def hidden(v0):
                    for v in range(v0, v0 + 4):
                        act.wait_ge(*hp_ready(g, v + 1))
                        if v >= 4:
                            act.wait_ge(*mo_mm(g, v - 3))
                        act.activation(ge[:, v % 4, :], eb[v % 2], ACT.Gelu, bias=C("b1", v // 2, 1)
                                       ).then_inc(ge_ready.sem, 1)
                    act.preload_act_table_set("natural_log_exp_and_others")

                yield 14.5
                if not_first(g):
                    act.wait_ge(*kz_landed(g - 1, 256))
                hidden(0)
                act.wait_ge(*ls_ready(g, 1))
                act.activation(rt[:, 1, :], rt[:, 0, :], ACT.Exp).then_inc(le_ready.sem, 1)
                yield 38.5
                hidden(4)
                yield 53
                act.wait_ge(*mo_mm(g, 8))
                act.activation(aF[:, :], eb[2], ACT.Copy).then_inc(moF_ready.sem, 1)
                yield PREP0 + 2
                square(g, 2, sqR[:, :], xcR[:, :])
                yield PREP0 + 9.5
                act.wait_ge(*xaT_ready(g, 1))
                act.activation(aF[:, :], eb[0], ACT.Copy).then_inc(xaF_ready.sem, 1)
                yield PREP0 + 14.5
                act.wait_ge(*xaT_ready(g, 2))
                act.activation(nF[:, :], eb[1], ACT.Identity, bias=C("beta"), scale=C("gamma")
                               ).then_inc(xaF_ready.sem, 1)
                for w in (*range(8), *range(12, 16)):
                    kind, i = divmod(w, 4)
                    yield (PREP0 + 18 if w < 12 else PREP0 + 24) + 1.3 * w
                    act.wait_ge(*pj_ready(g, w + 1))
                    if w == 0 and not_first(g):
                        act.wait_ge(*sc_ready(g - 1, 32))
                    if w == 12 and not_first(g):
                        act.wait_ge(*fo_ready(g - 1, 1))
                    if kind == 0:
                        m = act.activation(qF[:, i, :], eb[w % RING], ACT.Copy, scale=HEAD_DIM ** -0.5)
                    elif kind == 1:
                        m = act.activation(kF[:, i, :], eb[w % RING], ACT.Copy)
                    else:
                        m = act.activation(thg[:, i, :], eb[w % RING], ACT.Tanh, bias=half_bg[:, i % 2:i % 2 + 1],
                                           scale=0.5)
                    m.then_inc(pjA_done.sem, 1)

            def attention(g):
                for w in range(32):
                    yield ATT0 + ATT_DT * w + 2
                    act.wait_ge(*nmx_ready(g, w + 1))
                    if w >= RING:
                        act.wait_ge(*ot_done(g, w - RING + 1))
                    for c in range(2):
                        act.activation(prob[:, w % RING, c, :], bb[w % 2][:, c * SEQ:(c + 1) * SEQ], ACT.Exp,
                                       bias=nmx[:, w % 4, c:c + 1], accum_out=rsum[:, w % 4, c:c + 1]
                                       ).then_inc(exp_done.sem, 1)
                yield ATT1 + 4
                act.wait_ge(*fo_ready(g, 1))
                act.activation(aS[:, :], bb[0], ACT.Identity, bias=C("bf")).then_inc(foF_ready.sem, 1)
                yield BIN0 + 2
                square(g, 3, sqS[:, :], xcS[:, :])
                yield BIN0 + 10.5
                act.wait_ge(*xfT_ready(g, 1))
                act.activation(aS[:, :], bb[0], ACT.Copy).then_inc(xfF_ready.sem, 1)
                act.activation(xb[:, :], bb[0], ACT.Sign).then_inc(xfF_ready.sem, 1)
                for w in range(D):
                    yield BIN0 + 15.5 + BIN_DT * w
                    act.wait_ge(*w_ready(g, w + 1))
                    if w >= RING:
                        act.wait_ge(*red_done(g, w - RING + 1))
                    act.activation(sg[:, w % RING, :], bb[w % 2], ACT.Sign).then_inc(sg_ready.sem, 1)
                yield END
                act.wait_ge(*red_done(g, D))
                act.activation(aS[:, :], bb[2], ACT.Identity, bias=0.0, scale=C("scale")).then_inc(yF_ready.sem, 1)

            act.wait_ge(loaded.sem, 16 * LOADS)
            act.activation(negA[:, :], C("Alog"), ACT.Exp).then_inc(prepared.sem, 1)
            act.wait_ge(prepared.sem, PREPARED)
            iterations(act.Fori, scan, experts, attention)

        @block.vector
        def _(dve):
            tt, ts, stt, red = dve.tensor_tensor, dve.tensor_scalar, dve.scalar_tensor_tensor, dve.tensor_reduce
            steps = {}

            def link(chain, g, ins):
                steps[chain] = steps.get(chain, 0) % chain.per + 1
                ins.then_inc(chain.sem, 1)
                dve.wait_ge(*chain(g, steps[chain]))

            def tiles(ap):
                return ap.rearrange("p (k d) -> p k d", k=TILES)

            def centre(chain, g, i, h, xc, st):
                link(chain, g, red(st[:, 0, :], tiles(h), AX.X, ALU.add))
                stt(tiles(xc), bcast(st[:, 0, :], D), -1.0 / D, tiles(h), ALU.mult, ALU.add).then_inc(ln_xc[i].sem, 1)

            def square_sum(g, i, sq, st):
                dve.wait_ge(*ln_sq[i](g, 1))
                red(st[:, 1, :], tiles(sq), AX.X, ALU.add).then_inc(ln_var[i].sem, 1)

            def normalise(g, i, x, xc, st):
                dve.wait_ge(*ln_rs[i](g, 2))
                return stt(tiles(x), tiles(xc), float(D) ** 0.5, bcast(st[:, 2, :], D), ALU.mult, ALU.mult)

            def normalise_again(g, i, xn, x, st):
                dve.wait_ge(*ln_rs[i](g, 6))
                return tt(tiles(xn), tiles(x), bcast(st[:, 5, :], D), ALU.mult)

            def clip(g, i, x, src, bias):
                ts(x, src, bias, None, ALU.add).then_inc(lin_ready.sem, 1)
                dve.wait_ge(*lin_ready(g, i + 1))
                ts(um[:, i % 2, :], x, SOFTPLUS_CAP, None, ALU.min).then_inc(um_ready.sem, 1)

            def softplus(g, i, x):
                dve.wait_ge(*sl_ready(g, i + 1))
                return tt(x, x, um[:, i % 2, :], ALU.max)

            def scan(g):
                def weigh_b(k):
                    d = k // STATES
                    dve.wait_ge(*b_ready(g, k + 1))
                    dve.wait_ge(*du_ready(g, d + 1))
                    tt(bx[:, k % 2, :], du[:, d, :], mb[0], ALU.mult).then_inc(bx_done.sem, 1)

                yield 0
                dve.wait_ge(*emb_landed(g, 16 * TILES))
                if not_first(g):
                    dve.wait_ge(*h1_ready(g - 1, 1))
                tt(hM[:, :], emb[:, :], C("pe"), ALU.add).then_inc(emb_used.sem, 1)
                yield 1
                dve.wait_ge(*emb_used(g, 1))
                centre(chain_m, g, 0, hM[:, :], xcM[:, :], stM)
                yield 4
                square_sum(g, 0, sqM[:, :], stM)
                yield 7
                link(chain_m, g, normalise(g, 0, xlM[:, :], xcM[:, :], stM))
                yield 12
                normalise_again(g, 0, xnM[:, :], xlM[:, :], stM).then_inc(xn_ready.sem, 1)
                link(chain_m, g, tt(hM[:, :], hM[:, :], xlM[:, :], ALU.add))
                for d in range(2):
                    yield 21 + 1.5 * d
                    dve.wait_ge(*upre_ready(g, d + 1))
                    clip(g, d, u[:, d, :], mb[d], C("bc", d, 1))
                for d in range(2):
                    yield 24.5 + 1.5 * d
                    softplus(g, d, u[:, d, :]).then_inc(u_ready.sem, 1)
                dve.wait_ge(*u_ready(g, 2))
                for d in range(2):
                    yield 30 + 5 * d
                    dve.wait_ge(*hi_ready(g, d + 1))
                    if d:
                        dve.wait_ge(*sx_ready(g, 1))
                    for j in range(2):
                        i = stt(r1[:, j * N:(j + 1) * N], hi[:, j * N:(j + 1) * N], C("n1", rows=96),
                                mb[j][0:96, :], ALU.mult, ALU.add)
                    i.then_inc(r1_ready.sem, 1)
                    yield 33 + 5 * d
                    dve.wait_ge(*r1_ready(g, d + 1))
                    dve.wait_ge(*mid_ready(g, d + 1))
                    stt(SX[:, d, :], mid, C("n2", rows=96), r1, ALU.mult, ALU.add).then_inc(sx_ready.sem, 1)
                for d in range(2):
                    yield 38 + d
                    if d == 0:
                        dve.wait_ge(*sx_ready(g, 2))
                    dve.wait_ge(*dpre_ready(g, d + 1))
                    clip(g, 2 + d, delta[:, d, :], mb[d], C("bdt", d, 1))
                yield 40.5
                for d in range(2):
                    ts(acc[:, d, :], u[:, d, :], C("Dskip", d, 1), None, ALU.mult).then_inc(acc_init.sem, 1)
                for d in range(2):
                    yield 41.5 + d
                    softplus(g, 2 + d, delta[:, d, :]).then_inc(delta_ready.sem, 1)
                    dve.wait_ge(*delta_ready(g, d + 1))
                    tt(du[:, d, :], delta[:, d, :], u[:, d, :], ALU.mult).then_inc(du_ready.sem, 1)
                yield STATE0
                weigh_b(0)
                for k in range(2 * STATES):
                    d, turn = k // STATES, slice(None, None, -1 if k >= STATES else 1)
                    yield STATE0 + STATE_DT * k + 0.5
                    dve.wait_ge(*dA_ready(g, k + 1))
                    dve.wait_ge(*bx_done(g, k + 1))
                    dve.tensor_tensor_scan(hs[:, k % 2, turn], dA[:, d, k % STATES % RING, turn], bx[:, k % 2, turn],
                                           0.0, ALU.mult, ALU.add).then_inc(h_done.sem, 1)
                    if k + 1 < 2 * STATES:
                        yield STATE0 + STATE_DT * k + 1
                        weigh_b(k + 1)
                    yield STATE0 + STATE_DT * k + 1.8
                    dve.wait_ge(*c_ready(g, k + 1))
                    dve.wait_ge(*h_done(g, k + 1))
                    if k >= RING:
                        dve.wait_ge(*acc_done(g, k - RING + 1))
                    tt(pC[:, k % RING, :], hs[:, k % 2, :], mb[1], ALU.mult).then_inc(p_done.sem, 1)
                yield TAIL0 + 2
                dve.wait_ge(*acc_done(g, 2 * STATES))
                dve.wait_ge(*th_ready(g, 3))
                dve.wait_ge(*z1_ready(g, 1))
                stt(sy[:, 0, :], th[:, 0, :], 1.0, acc[:, 0, :], ALU.add, ALU.mult)
                link(chain_m, g, stt(sy[:, 1, :], th[:, 1, :], 1.0, acc[:, 1, :], ALU.add, ALU.mult))
                stt(th[:, 2, :], th[:, 2, :], 1.0, z1[:, :], ALU.add, ALU.mult)
                link(chain_m, g, tt(sy[:, 0, :], sy[:, 0, :], sy[:, 1, :], ALU.add))
                stt(mF, sy[:, 0, :], 0.25, th[:, 2, :], ALU.mult, ALU.mult).then_inc(m_ready.sem, 1)
                yield TAIL0 + 5
                dve.wait_ge(*mT_ready(g, 1))
                tt(hB[:, :], hM[:, :], mb[0], ALU.add).then_inc(h1_ready.sem, 1)

            def experts(g):
                e8 = EXPERTS

                def t3(j):
                    return rt[:, j, :].rearrange("p (k e) -> p k e", e=e8)

                yield 0.2
                dve.wait_ge(*h1_ready(g, 1))
                if not_first(g):
                    dve.wait_ge(*hS_ready(g - 1, 1))
                link(chain_e, g, dve.tensor_copy(hR[:, :], hB[:, :]))
                yield 1
                centre(chain_e, g, 1, hR[:, :], xcR[:, :], stR)
                yield 4
                square_sum(g, 1, sqR[:, :], stR)
                yield 7.5
                normalise(g, 1, xR[:, :], xcR[:, :], stR).then_inc(xm_ready.sem, 1)
                dve.wait_ge(*xm_ready(g, 1))
                link(chain_e, g, tt(hR[:, :], hR[:, :], xR[:, :], ALU.add))
                mx, sm, ri, m1, i1, m2, i2, dn, rd = (rs8[:, j, :] for j in range(9))
                logits = eb[2][:, 0:TILES * e8].rearrange("p (k e) -> p k e", e=e8)
                iota = C("iota").rearrange("p (k e) -> p k e", e=e8)
                yield 13
                dve.wait_ge(*lg_ready(g, 1))
                link(chain_e, g, red(mx, logits, AX.X, ALU.max))
                tt(t3(0), logits, bcast(mx, e8), ALU.subtract).then_inc(ls_ready.sem, 1)
                yield 20
                dve.wait_ge(*le_ready(g, 1))
                link(chain_e, g, red(sm, t3(1), AX.X, ALU.add))
                link(chain_e, g, dve.reciprocal(ri, sm))
                link(chain_e, g, tt(t3(2), t3(1), bcast(ri, e8), ALU.mult))
                for m, i, onehot, rest in ((m1, i1, 4, 6), (m2, i2, 5, None)):
                    yield 21 if rest else 23
                    probs = t3(2) if rest else t3(6)
                    link(chain_e, g, red(m, probs, AX.X, ALU.max))
                    link(chain_e, g, tt(t3(3), probs, bcast(m, e8), ALU.is_equal))
                    link(chain_e, g, stt(t3(3), t3(3), -float(e8), iota, ALU.mult, ALU.add))
                    yield 22 if rest else 24
                    link(chain_e, g, red(i, t3(3), AX.X, ALU.min))
                    link(chain_e, g, stt(t3(onehot), iota, -float(e8), bcast(i, e8), ALU.add, ALU.is_equal))
                    if rest:
                        link(chain_e, g, stt(t3(rest), t3(onehot), -2.0, t3(2), ALU.mult, ALU.add))
                yield 25
                link(chain_e, g, tt(dn, m1, m2, ALU.add))
                link(chain_e, g, ts(dn, dn, 1e-12, None, ALU.max))
                link(chain_e, g, dve.reciprocal(rd, dn))
                yield 26
                tt(t3(4), t3(4), bcast(m1, e8), ALU.mult)
                link(chain_e, g, tt(t3(5), t3(5), bcast(m2, e8), ALU.mult))
                link(chain_e, g, tt(t3(4), t3(4), t3(5), ALU.add))
                tt(comb[:, :].rearrange("p (k e) -> p k e", e=e8), t3(4), bcast(rd, e8), ALU.mult
                   ).then_inc(comb_ready.sem, 1)
                yield 28
                dve.wait_ge(*cTp_ready(g, 1))
                dve.tensor_copy(cT, eb[0][0:16, :]).then_inc(cT_ready.sem, 1)
                for v in range(8):
                    yield (28.5, 30.5, 32.5, 35, 44.5, 46, 47.5, 50)[v]
                    dve.wait_ge(*ge_ready(g, v + 1))
                    dve.wait_ge(*cb_ready(g, v + 1))
                    tt(ge[:, v % 4, :], ge[:, v % 4, :], eb[1 - v % 2], ALU.mult).then_inc(gg_ready.sem, 1)
                yield PREP0
                dve.wait_ge(*moT_ready(g, 1))
                link(chain_e, g, tt(hR[:, :], hR[:, :], eb[0], ALU.add))
                centre(chain_e, g, 2, hR[:, :], xcR[:, :], stR)
                yield PREP0 + 3.5
                square_sum(g, 2, sqR[:, :], stR)
                yield PREP0 + 7
                normalise(g, 2, xR[:, :], xcR[:, :], stR).then_inc(xa_ready.sem, 1)
                dve.wait_ge(*xa_ready(g, 1))
                tt(hR[:, :], hR[:, :], xR[:, :], ALU.add).then_inc(hR_done.sem, 1)
                yield PREP0 + 12
                normalise_again(g, 2, xnR[:, :], xR[:, :], stR).then_inc(xa_ready.sem, 1)
                for i in range(4):
                    yield PREP0 + 18 + 1.3 * (8 + i)
                    dve.wait_ge(*pj_ready(g, 8 + i + 1))
                    if i == 0 and not_first(g):
                        dve.wait_ge(*vs_ready(g - 1, 32))
                    dve.tensor_copy(vT[:, i, :], eb[(8 + i) % RING]).then_inc(pjV_done.sem, 1)

            def attention(g):
                def row_max(w):
                    dve.wait_ge(*sc_ready(g, w + 1))
                    red(nmx[:, w % 4, :], bb[w % 2].rearrange("p (c t) -> p c t", c=2), AX.X, ALU.max,
                        negate=True).then_inc(nmx_ready.sem, 1)

                def scale_v(w):
                    sb_, a, r = w // 8, w // 4 % 2, w % 4
                    s, b = divmod(sb_, 2)
                    h = 4 * b + r
                    dve.wait_ge(*exp_done(g, 2 * w + 2))
                    dve.reciprocal(rinv[:, w % 4, :], rsum[:, w % 4, :]).then_inc(rinv_ready.sem, 1)
                    if w >= RING:
                        dve.wait_ge(*ot_done(g, w - RING + 1))
                    dve.wait_ge(*rinv_ready(g, w + 1))
                    v = vT[:, 2 * s + a, :].rearrange("p (c m) -> p c m", c=2)[:, :, h * HEAD_DIM:(h + 1) * HEAD_DIM]
                    tt(vs[:, w % RING, :, :], v, bcast(rinv[:, w % 4, :], HEAD_DIM), ALU.mult
                       ).then_inc(vs_ready.sem, 1)

                yield 0
                dve.wait_ge(*hR_done(g, 1))
                if not_first(g):
                    dve.wait_ge(*stored(g, 0))
                dve.tensor_copy(hS[:, :], hR[:, :]).then_inc(hS_ready.sem, 1)
                dve.wait_ge(*pjV_done(g, 4))
                for w in range(33):
                    if w < 32:
                        yield ATT0 + ATT_DT * w + 1.2
                        row_max(w)
                    if w >= 1:
                        yield ATT0 + ATT_DT * (w - 1) + 3.2
                        scale_v(w - 1)
                    if w >= 8 and w % 8 == 0:
                        i = w // 8 - 1
                        yield ATT0 + ATT_DT * (w - 1) + 4
                        dve.wait_ge(*ot_done(g, 8 * i + 8))
                        dve.wait_ge(*pjA_done(g, 8 + i + 1))
                        stt(og[:, i, :], thg[:, i, :], 1.0, bb[2], ALU.add, ALU.mult).then_inc(og_ready.sem, 1)
                yield BIN0
                dve.wait_ge(*foT_ready(g, 1))
                link(chain_s, g, tt(hS[:, :], hS[:, :], bb[1], ALU.add))
                centre(chain_s, g, 3, hS[:, :], xcS[:, :], stS)
                yield BIN0 + 3.5
                square_sum(g, 3, sqS[:, :], stS)
                yield BIN0 + 7.5
                normalise(g, 3, xS[:, :], xcS[:, :], stS).then_inc(xf_ready.sem, 1)
                yield BIN0 + 13.5
                dve.wait_ge(*gp_ready(g, 1))
                ts(G[:, :], bb[1][0:96, :], C("pb", rows=96), 0.0, ALU.add, ALU.is_gt).then_inc(G_ready.sem, 1)
                for w in range(D):
                    yield BIN0 + 16 + BIN_DT * w
                    if w == 0:
                        dve.wait_ge(*xfF_ready(g, 2))
                    dve.wait_ge(*sg_ready(g, w + 1))
                    tt(sg[:, w % RING, :], sg[:, w % RING, :], xb[:, :], ALU.mult).then_inc(zz_ready.sem, 1)
                yield END + 2
                dve.wait_ge(*yT_ready(g, 1))
                tt(outT[:, :], hS[:, :], bb[0], ALU.add).then_inc(out_ready.sem, 1)

            dve.wait_ge(loaded.sem, 16 * LOADS)
            dve.memset(dA[:, :, :, :], 0.0).then_inc(prepared.sem, 1)
            ts(half_bg[:, :], C("bg"), 0.5, None, ALU.mult).then_inc(prepared.sem, 1)
            ts(half_Wf[:, :, :].rearrange("p b d -> p (b d)"), C("Wf"), 0.5, None, ALU.mult).then_inc(prepared.sem, 1)
            dve.wait_ge(prepared.sem, 3 + 1 + 1)
            ts(negA[:, :], negA[:, :], -1.0, None, ALU.mult).then_inc(prepared.sem, 1)
            for d in range(2):
                dve.tensor_copy(Wdt[:, d, :], mb[d][:, 0:P]).then_inc(prepared.sem, 1)
            n = 3 + 1 + 1 + 3
            for q in range(8):
                w = kz[0:96, q, :]
                dve.tensor_copy(sg[0:96, 0, :], w).then_inc(prepared.sem, 1)
                dve.wait_ge(prepared.sem, n + 1)
                stt(w, sg[0:96, 0, :], C("w_n1", rows=96), w, ALU.mult, ALU.add).then_inc(prepared.sem, 1)
                dve.wait_ge(prepared.sem, n + 2)
                dve.tensor_copy(sg[0:96, 1, :], w).then_inc(prepared.sem, 1)
                dve.wait_ge(prepared.sem, n + 3)
                stt(w, sg[0:96, 1, :], C("w_n2", rows=96), w, ALU.mult, ALU.add).then_inc(prepared.sem, 1)
                dve.wait_ge(prepared.sem, n + 4)
                n += 4
                for s in range(2):
                    ts(Wt[:, 8 * q:8 * q + 8, s * D:(s + 1) * D], w.rearrange("p (o i) -> p o i", i=D),
                       C("w_s", s, 1, 96), None, ALU.mult).then_inc(prepared.sem, 1)
                n += 2
            dve.wait_ge(prepared.sem, n)
            dve.memset(kz[:, :, :], 0.0).then_inc(prepared.sem, 1)
            assert n + 1 == PREPARED, n
            iterations(dve.Fori, scan, experts, attention)
            assert all(steps[c] == c.per for c in steps), {k: v for k, v in zip("mes", steps.values())}


def layout(inputs):
    import numpy as np

    f = np.float32
    c = np.zeros((P, NCONST), f)

    def at(name, i=0, w=None):
        a, width = COL[name]
        w = width if w is None else w
        return c[:, a + i * w:a + (i + 1) * w]

    L0 = {k[len("L0_attn_"):]: np.asarray(v) for k, v in inputs.items() if k.startswith("L0_attn_")}
    E0 = {k[len("L0_ffn_"):]: np.asarray(v) for k, v in inputs.items() if k.startswith("L0_ffn_")}
    L1 = {k[len("L1_attn_"):]: np.asarray(v) for k, v in inputs.items() if k.startswith("L1_attn_")}
    E1 = {k[len("L1_ffn_"):]: np.asarray(v) for k, v in inputs.items() if k.startswith("L1_ffn_")}
    at("ident")[:] = np.eye(P)
    for s in range(2):
        r = slice(s * D, s * D + D)
        at("Wp")[r, r] = L0["Wp"]
        for d, x in enumerate("fb"):
            at("Wc", d, 128)[r, r] = L0["Wc" + x].T
            for j in range(2):
                for part in range(3):
                    k = part * 32 + s * 16
                    at("Wx", 2 * d + j, 96)[r, k:k + 16] = L0["Wdbc_" + x][:, 16 + 16 * j:32 + 16 * j]
            rr = slice(s * 16, s * 16 + 16)
            at("dt_in" if d == 0 else "dt_in_b")[rr, r] = L0["Wdbc_" + x][:, :16].T
            at("dt_out", d, 128)[rr, r] = L0["Wdt_" + x]
            at("bc")[r, d] = L0["bc" + x]
            at("bdt")[r, d] = L0["bdt_" + x]
            at("Dskip")[r, d] = L0["D_" + x]
            at("Alog", d, 16)[r] = L0["Alog_" + x]
        for name, v in (("ln_g", L0["ln_g"]), ("ln_b", L0["ln_b"]), ("bp", L0["bp"]), ("gamma", L1["ln_gamma"]),
                        ("beta", L1["ln_beta"]), ("bf", L1["b_final"])):
            at(name)[r, 0] = v
        for ep in range(4):
            for e in range(2):
                at("W1", 2 * ep + s, 128)[r, e * D:(e + 1) * D] = E0["w1"][2 * ep + e]
        at("b2")[s * 8:s * 8 + 8, r] = E0["b2"]
        at("router")[r, s * 8:s * 8 + 8] = E0["router_w"].T
        for b in range(2):
            m = slice(b * P, b * P + P)
            at("Wq", 2 * s + b, 128)[r] = L1["W_qkv"][m].T
            at("Wk", 2 * s + b, 128)[r] = L1["W_qkv"][256:][m].T
            at("Wg", 2 * s + b, 128)[r] = L1["W_gate"][m].T
        at("Wv", s, 256)[r] = L1["W_qkv"][512:].T
        for part in range(3):
            k = part * 16 + s * 8
            at("proj")[r, k:k + 8] = E1["proj_w"].T
            at("pb")[k:k + 8, 0] = E1["proj_b"]
            at("w_s")[k:k + 8, s] = 1
        for q in range(4):
            k = q * 32 + s * 16
            at("scale")[k:k + 16, 0] = E1["scale"][0, 0, q * 16:(q + 1) * 16]
            for o in range(16):
                at("perm")[k + o, s * D + q * 16 + o] = 1
    at("pb")[48:96] = -1
    for ep in range(4):
        for e in range(2):
            at("W2", ep, 64)[e * D:(e + 1) * D] = E0["w2"][2 * ep + e]
            at("b1")[e * D:(e + 1) * D, ep] = E0["b1"][2 * ep + e]
    for b in range(2):
        at("bg")[:, b] = L1["b_gate"][b * P:(b + 1) * P]
        at("Wf", b, 64)[:] = L1["W_final"][:, b * P:(b + 1) * P].T
    at("n1")[32:96] = -1
    at("n2")[64:96] = -1
    at("w_n1")[16:48] = -1
    at("w_n2")[32:48] = -1
    at("mhalf")[:] = -0.5
    at("eps64")[:] = D * EPS
    at("eps")[:] = EPS
    at("iota")[:] = np.tile(np.arange(EXPERTS, dtype=f), TILES)
    pos = np.arange(SEQ, dtype=f)[:, None]
    dim = np.arange(D)
    inv = np.power(f(10000.0), -((dim - dim % 2).astype(f) / f(D)), dtype=f)
    angle = (pos * inv).astype(f)
    pe = np.where(dim % 2 == 0, np.sin(angle), np.cos(angle)).astype(f)
    at("pe").reshape(P, 2, 2, 2, D)[:] = pe.reshape(2, P, D).transpose(1, 0, 2)[:, None, :, None, :]

    one = 0x3F80
    sel = np.zeros((96, STATES, P), np.uint16)
    for part in range(3):
        for s in range(2):
            for n in range(STATES):
                sel[part * 32 + s * 16 + n, n, s * D:(s + 1) * D] = one
    ones = np.zeros((P, 16, 32), np.uint16)
    for s in range(2):
        for j in range(16):
            ones[s * D:(s + 1) * D, j, s * 16 + j] = one
    w = np.zeros((96, 8, N), f)
    wt = E1["weight"][0].transpose(0, 2, 1).reshape(EXPERTS, 8, N)
    for k in range(6):
        w[k * 8:k * 8 + 8] = wt
    x = np.asarray(inputs["x"]).astype(np.int32)
    ids = np.zeros((P, (GROUPS + 1) * TILES), np.int32)
    ids[:, :GROUPS * TILES] = x.reshape(GROUPS, 2, 2, 2, P).transpose(4, 0, 1, 3, 2).reshape(P, -1)
    return {"table": np.ascontiguousarray(inputs["L0_tok_W"]), "ids": ids, "consts": c, "selectors": sel,
            "ones_sel": ones, "w_exp": w}


def kernel(**inputs):
    import numpy as np
    from concourse import bacc
    from concourse.bass_utils import run_bass_kernel_spmd

    nc = bacc.Bacc("TRN2", target_bir_lowering=False, num_devices=1)
    arrays = layout(inputs)
    args = [nc.dram_tensor(k, a.shape, mybir.dt.from_np(a.dtype), kind="ExternalInput").ap()
            for k, a in arrays.items()]
    args.append(nc.dram_tensor("out", (GROUPS * P, N), F32, kind="ExternalOutput").ap())
    build_tower(nc, *args)
    r = run_bass_kernel_spmd(nc, [arrays], core_ids=[0])
    got = np.asarray(r.results[0]["out"]).reshape(GROUPS, P, 2, 2, 2, D)
    return got.transpose(0, 2, 4, 3, 1, 5).reshape(BATCH, SEQ, D)
```

```python
from contextlib import ExitStack
from itertools import chain

import concourse.bass as bass
from concourse import mybir

F32 = mybir.dt.float32
BF16 = mybir.dt.bfloat16
I32 = mybir.dt.int32
U16 = mybir.dt.uint16
ALU = mybir.AluOpType
ACT = mybir.ActivationFunctionType
AX = mybir.AxisListType

P = 128
D = 64
SEQ = 256
BATCH = 32
GROUPS = 8
N = 512
TILES = 8
STATES = 16
DT_RANK = 16
EXPERTS = 8
HEADS = 8
HEAD_DIM = 32
EPS = 1e-5
STATE0, STATE_DT = 26, 2.5
TAIL0 = 108
PREP0 = 58
EMB0 = 98
ATT0, ATT_DT = 2, 1.7
ATT1 = ATT0 + ATT_DT * 35
BIN0, BIN_DT = ATT1 + 8, 0.7
END = BIN0 + 15 + BIN_DT * (D + 3) + 1
SCAN_PACE = (113.0, [10.0, 21.3, 37.2, 46.1, 57.3, 77.2, 85.3, 98.1, 110.2, 121.3, 151.2])
EXPERTS_PACE = (116.0, [6.0, 19.9, 24.8, 38.8, 44.6, 59.6, 73.8, 81.8, 96.4, 102.8, 127.4])
ATTENTION_PACE = (135.4, [0.0, 17.9, 33.2, 45.3, 55.7, 69.3, 85.5, 96.2, 108.6, 120.8, 148.7])
SOFTPLUS_CAP = 40.0
RING = 3
RING_S = 4

_WIDTHS = [
    ("ident", 128), ("perm", 128), ("Wp", 128), ("Wc", 256), ("Wx", 4 * 96), ("dt_in", 128), ("dt_out", 256),
    ("dt_in_b", 128), ("W1", 8 * 128), ("W2", 4 * 64), ("b2", 128), ("router", 16), ("Wq", 512), ("Wk", 512),
    ("Wv", 512), ("Wg", 512), ("Wf", 128), ("proj", 96), ("pe", 512), ("iota", 64), ("mhalf", 8), ("mone", 2), ("eps", 8),
    ("ln_g", 1), ("ln_b", 1), ("bp", 1), ("bc", 2), ("bdt", 2), ("Dskip", 2), ("Alog", 32), ("b1", 4),
    ("gamma", 1), ("beta", 1), ("bg", 2), ("bf", 1), ("scale", 1), ("pb", 1), ("n1", 1), ("n2", 1),
    ("w_n1", 1), ("w_n2", 1), ("w_s", 2),
]
COL, _at = {}, 0
for _name, _w in _WIDTHS:
    COL[_name] = (_at, _w)
    _at += _w
NCONST = _at


class Signal:

    def __init__(self, sem, per, seed=0):
        self.sem, self.per, self.seed = sem, per, seed

    def __call__(self, g, k):
        return self.sem, g * self.per + (k + self.seed)


def weave(*stages):
    at = [(next(s), i) for i, s in enumerate(stages)]
    while at:
        slot, i = min(at)
        at.remove((slot, i))
        following = next(stages[i], None)
        if following is not None:
            at.append((max(following, slot), i))


def paced(stage, pace):
    last, times = pace
    for slot in stage:
        x = slot / last * (len(times) - 1)
        k = min(int(x), len(times) - 2)
        yield times[k] + (x - k) * (times[k + 1] - times[k])


def iterations(fori, embed, scan, experts, attention, *once):
    weave(embed(0))
    weave(paced(scan(0), SCAN_PACE), paced(embed(1), EXPERTS_PACE), *once)
    weave(paced(scan(1), SCAN_PACE), paced(chain(experts(0), embed(2)), EXPERTS_PACE))
    with fori(2, GROUPS) as i:
        weave(paced(scan(i), SCAN_PACE), paced(chain(experts(i - 1), embed(i + 1)), EXPERTS_PACE),
              paced(attention(i - 2), ATTENTION_PACE))
    weave(paced(experts(GROUPS - 1), EXPERTS_PACE), paced(attention(GROUPS - 2), ATTENTION_PACE))
    weave(attention(GROUPS - 1))


def not_first(g):
    return not isinstance(g, int) or g > 0


def bcast(ap, n):
    p, m = ap.shape
    return ap.unsqueeze(2).to_broadcast([p, m, n])


def build_tower(nc, table, ids, consts, selectors, ones_sel, w_exp, out):
    with ExitStack() as ctx:
        def sb(name, shape, dt=F32):
            return ctx.enter_context(nc.sbuf_tensor(name, shape, dt))

        signals = {}

        def sig(name, per, seed=0):
            s = Signal(ctx.enter_context(nc.semaphore(name)), per, seed)
            signals[name] = s
            return s

        cst = sb("cst", [P, NCONST])

        def C(name, i=0, w=None, rows=P):
            at, width = COL[name]
            w = width if w is None else w
            return cst[0:rows, at + i * w:at + (i + 1) * w]

        ident = C("ident")
        sel = sb("sel", [96, STATES, P], BF16)
        ones_w = sb("ones_w", [P, 16, 32], BF16)
        Wt = sb("Wt", [96, D, P], BF16)
        idx_all = sb("idx_all", [P, (GROUPS + 1) * TILES], I32)
        idx = sb("idx", [P, TILES], I32)
        negA = sb("negA", [P, 2 * STATES])
        Wdt = sb("Wdt", [P, 2, P])
        half_bg = sb("half_bg", [P, 2])
        half_Wf = sb("half_Wf", [P, 2, D])

        hN = sb("hN", [P, N])
        z1N = sb("z1N", [P, N])
        stM = sb("stM", [P, 8, TILES])
        hM = sb("hM", [P, N])
        z1 = sb("z1", [P, N])
        um = sb("um", [P, 2, N])
        u = sb("u", [P, 2, N])
        r1 = um[0:96, :, :].rearrange("p j n -> p (j n)")
        SX = sb("SX", [96, 2, 2 * N], BF16)
        delta = sb("delta", [P, 2, N])
        du = sb("du", [P, 2, N])
        dA = sb("dA", [P, 2, RING, N])
        bx = sb("bx", [P, 2, N])
        hs = sb("hs", [P, 2, N])
        hi, mid = (bx[0:96, j, :].bitcast(BF16) for j in range(2))
        pC = sb("pC", [P, RING, N])
        acc = sb("acc", [P, 2, N])
        th, sy, mF = pC, bx, hs[:, 0, :]

        hR = sb("hR", [P, N])
        xcR, sqR = sb("xcR", [P, N]), sb("sqR", [P, N])
        xR, xnR = sqR, xcR
        stR = sb("stR", [P, 8, TILES])
        aF = sb("aF", [P, N])
        nF = sb("nF", [P, N])
        xcM, sqM, xlM, xnM, xnF = xcR[:, :], sqR[:, :], sqR[:, :], xcR[:, :], aF[:, :]
        rt = sb("rt", [P, 7, TILES * EXPERTS])
        rs8 = sb("rs8", [P, 9, TILES])
        comb = sb("comb", [P, TILES * EXPERTS])
        cT = nF[0:16, :]
        ge = sb("ge", [P, 8, N])
        qF = sb("qF", [P, 4, N])
        kF = ge[:, 0:4, :]
        kz = sb("kz", [P, 16, N])
        vT = sb("vT", [P, 4, N])
        thg = sb("thg", [P, 4, N])
        og = thg

        hS = sb("hS", [P, N])
        xcS, sqS = sb("xcS", [P, N]), sb("sqS", [P, N])
        xS = sqS
        stS = sb("stS", [P, 8, TILES])
        aS = sb("aS", [P, N])
        nmx = sb("nmx", [P, RING_S, 2])
        rsum = sb("rsum", [P, RING_S, 2])
        rinv = sb("rinv", [P, RING_S, 2])
        spare = sb("spare", [P, TILES])
        prob = sb("prob", [P, RING_S, 2, SEQ])
        vs = sb("vs", [P, RING_S, 2, HEAD_DIM])
        xb = xcS[:, 0:N // 2].bitcast(BF16)
        G = xcS[0:96, N // 2:N].bitcast(BF16)
        sg = prob[:, :, 0, :].bitcast(BF16)
        outT = hS

        banks = [ctx.enter_context(nc.psum_tensor(f"ps{i}", [P, N], F32)) for i in range(8)]
        mb, eb, bb = ([b[:, :] for b in x] for x in (banks[0:2], banks[2:4], banks[4:8]))

        loaded = sig("loaded", 0)
        idx_loaded = sig("idx_loaded", 0)
        w_loaded = sig("w_loaded", 0)
        prepared = sig("prepared", 0)
        w_split = sig("w_split", 0)
        emb_landed = sig("emb_landed", 16 * TILES)
        idx_copied = sig("idx_copied", 1)
        pe_added = sig("pe_added", 1)
        h_moved = sig("h_moved", 1)
        z1_moved = sig("z1_moved", 1)
        h1_moved = sig("h1_moved", 1)
        chain_0, chain_m = sig("chain_0", 1), sig("chain_m", 2)
        chain_e, chain_s = sig("chain_e", 23), sig("chain_s", 2)
        ln_xc = [sig(f"ln_xc{i}", 1) for i in range(4)]
        ln_sq = [sig(f"ln_sq{i}", 1) for i in range(4)]
        ln_var = [sig(f"ln_var{i}", 1) for i in range(4)]
        ln_rs = [sig(f"ln_rs{i}", 6 if i in (0, 2) else 2) for i in range(4)]
        xl_ready = sig("xl_ready", 1)
        xn_ready = sig("xn_ready", 1)
        hN_ready = sig("hN_ready", 1)
        spare_done = sig("spare_done", 1)
        xnT_ready = sig("xnT_ready", 1)
        xnF_ready = sig("xnF_ready", 1)
        z1p_ready = sig("z1p_ready", 1)
        z1_ready = sig("z1_ready", 1)
        upre_ready = sig("upre_ready", 2)
        lin_ready = sig("lin_ready", 4)
        um_ready = sig("um_ready", 4)
        se_ready = sig("se_ready", 4)
        sl_ready = sig("sl_ready", 4)
        u_ready = sig("u_ready", 2)
        xp_ready = sig("xp_ready", 2)
        hi_ready = sig("hi_ready", 2)
        r1_ready = sig("r1_ready", 2)
        mid_ready = sig("mid_ready", 2)
        sx_ready = sig("sx_ready", 2)
        dpre_ready = sig("dpre_ready", 2)
        delta_ready = sig("delta_ready", 2)
        du_f_ready = sig("du_f_ready", 1)
        du_b_ready = sig("du_b_ready", 1)
        acc_init = sig("acc_init", 2)
        b_ready = sig("b_ready", 2 * STATES)
        c_ready = sig("c_ready", 2 * STATES)
        dA_ready = sig("dA_ready", 2 * STATES)
        bx_done = sig("bx_done", 2 * STATES)
        h_done = sig("h_done", 2 * STATES)
        p_done = sig("p_done", 2 * STATES)
        acc_done = sig("acc_done", 2 * STATES)
        th_ready = sig("th_ready", 3)
        m_ready = sig("m_ready", 1)
        mT_ready = sig("mT_ready", 1)
        h1_ready = sig("h1_ready", 1)

        xm_ready = sig("xm_ready", 1)
        xmT_ready = sig("xmT_ready", 1)
        xmF_ready = sig("xmF_ready", 1)
        lg_ready = sig("lg_ready", 1)
        ls_ready = sig("ls_ready", 1)
        le_ready = sig("le_ready", 1)
        comb_ready = sig("comb_ready", 1)
        cTp_ready = sig("cTp_ready", 1)
        cT_ready = sig("cT_ready", 1)
        hp_ready = sig("hp_ready", 8)
        cb_ready = sig("cb_ready", 8)
        ge_ready = sig("ge_ready", 8)
        gg_ready = sig("gg_ready", 8)
        mo_mm = sig("mo_mm", 8)
        moF_ready = sig("moF_ready", 1)
        moT_ready = sig("moT_ready", 1)
        xa_ready = sig("xa_ready", 1)
        xaa_ready = sig("xaa_ready", 1)
        hm_ready = sig("hm_ready", 1)
        xaT_ready = sig("xaT_ready", 2)
        xaF_ready = sig("xaF_ready", 2)
        pj_ready = sig("pj_ready", 16)
        pjA_done = sig("pjA_done", 12)
        pjV_done = sig("pjV_done", 4)
        kz_landed = sig("kz_landed", 16 * 16)
        sc_ready = sig("sc_ready", 32)
        nmx_ready = sig("nmx_ready", 32)
        exp_done = sig("exp_done", 64)
        rinv_ready = sig("rinv_ready", 32)
        vs_ready = sig("vs_ready", 32)
        ot_done = sig("ot_done", 32)
        og_ready = sig("og_ready", 4)
        fo_ready = sig("fo_ready", 1)
        foF_ready = sig("foF_ready", 1)
        foT_ready = sig("foT_ready", 1)
        xf_ready = sig("xf_ready", 1)
        xfT_ready = sig("xfT_ready", 1)
        xfF_ready = sig("xfF_ready", 2)
        gp_ready = sig("gp_ready", 1)
        G_ready = sig("G_ready", 1)
        w_ready = sig("w_ready", D)
        sg_ready = sig("sg_ready", D)
        zz_ready = sig("zz_ready", D)
        red_done = sig("red_done", D)
        yF_ready = sig("yF_ready", 1)
        yT_ready = sig("yT_ready", 1)
        hS_ready = sig("hS_ready", 1)
        hR_done = sig("hR_done", 1)
        out_ready = sig("out_ready", 1)
        stored = sig("stored", 16, seed=16)

        LOADS = 3
        PREPARED = 1 + 1 + 3 + 3
        W_SPLIT = 8 * 6 + 1

        block = ctx.enter_context(nc.Block())

        @block.sync
        def _(sp):
            sp.dma_start(idx_all[:, :], ids).then_inc(idx_loaded.sem, 16)
            sp.dma_start(cst[:, :], consts).then_inc(loaded.sem, 16)
            sp.dma_start(sel[:, :, :].bitcast(U16), selectors).then_inc(loaded.sem, 16)
            sp.dma_start(ones_w[:, :, :].bitcast(U16), ones_sel).then_inc(loaded.sem, 16)
            sp.dma_start(kz[0:96, 0:8, :], w_exp).then_inc(w_loaded.sem, 16)
            sp.sem_inc(stored.sem, 16)

            def embed(g):
                yield 0

            def scan(g):
                yield 0

            def experts(g):
                yield 80
                for i in range(4):
                    sp.wait_ge(*pjA_done(g, 4 + i + 1))
                    sp.wait_ge(w_split.sem, W_SPLIT)
                    if not_first(g):
                        sp.wait_ge(*sc_ready(g - 1, 32))
                    for r in range(4):
                        rows = slice(32 * r, 32 * r + 32)
                        sp.dma_start(kz[rows, 4 * i + r, :], kF[rows, i, :]).then_inc(kz_landed.sem, 16)

            def attention(g):
                yield END + 3
                sp.wait_ge(*out_ready(g, 1))
                start = g * P
                sp.dma_start(out[bass.ds(start, P), :], outT[:, :]).then_inc(stored.sem, 16)

            iterations(sp.Fori, embed, scan, experts, attention)
            sp.wait_ge(*stored(GROUPS, 0))
            sp.wait_ge(*emb_landed(GROUPS + 1, 0))

        @block.gpsimd
        def _(pool):
            def gather(k):
                pool.indirect_dma_start(hN[:, k * D:(k + 1) * D], None, table,
                                        bass.IndirectOffsetOnAxis(ap=idx[:, k:k + 1], axis=0)
                                        ).then_inc(emb_landed.sem, 16)

            def root(g, i, st):
                var, rs, t, v2, r2 = (st[:, j, :] for j in range(1, 6))
                done = ln_rs[i]
                pool.wait_ge(*ln_var[i](g, 1))
                pool.tensor_tensor(t, var, C("eps"), ALU.add).then_inc(done.sem, 1)
                pool.wait_ge(*done(g, 1))
                pool.tensor_tensor(rs, t, C("mhalf"), ALU.pow).then_inc(done.sem, 1)
                if done.per == 6:
                    pool.wait_ge(*done(g, 2))
                    pool.tensor_tensor(t, rs, rs, ALU.mult).then_inc(done.sem, 1)
                    pool.wait_ge(*done(g, 3))
                    pool.tensor_tensor(v2, t, var, ALU.mult).then_inc(done.sem, 1)
                    pool.wait_ge(*done(g, 4))
                    pool.tensor_tensor(v2, v2, C("eps"), ALU.add).then_inc(done.sem, 1)
                    pool.wait_ge(*done(g, 5))
                    pool.tensor_tensor(r2, v2, C("mhalf"), ALU.pow).then_inc(done.sem, 1)

            def tiles(ap):
                return ap.rearrange("p (k d) -> p k d", k=TILES)

            def normalise(g, i, x, xc, st):
                pool.wait_ge(*ln_rs[i](g, 2))
                return pool.tensor_tensor(tiles(x), tiles(xc), bcast(st[:, 2, :], D), ALU.mult)

            def normalise_again(g, i, xn, x, st):

                pool.wait_ge(*ln_rs[i](g, 6))
                return pool.tensor_tensor(tiles(xn), tiles(x), bcast(st[:, 5, :], D), ALU.mult)

            pool.wait_ge(idx_loaded.sem, 16)
            pool.tensor_copy(idx[:, :], idx_all[:, 0:TILES]).then_inc(idx_copied.sem, 1)
            pool.wait_ge(idx_copied.sem, 1)
            for k in range(TILES):
                gather(k)
            pool.wait_ge(loaded.sem, 16 * LOADS)

            def embed(g):
                yield EMB0 + 4.5
                root(g, 0, stM)
                normalise(g, 0, xlM, xcM, stM).then_inc(xl_ready.sem, 1)
                yield EMB0 + 8
                pool.wait_ge(*xl_ready(g, 1))
                normalise_again(g, 0, xnM, xlM, stM).then_inc(xn_ready.sem, 1)
                yield EMB0 + 10
                pool.tensor_tensor(hN[:, :], hN[:, :], xlM, ALU.add).then_inc(hN_ready.sem, 1)

            def scan(g):
                yield 0.5
                pool.wait_ge(*emb_landed(g, 16 * TILES))
                pool.tensor_copy(idx[:, :], idx_all[:, bass.ds(g * TILES + TILES, TILES)]).then_inc(idx_copied.sem, 1)
                pool.wait_ge(*idx_copied(g, 2))
                pool.wait_ge(*h_moved(g, 1))
                pool.tensor_tensor(spare[:, :], C("eps"), C("eps"), ALU.mult).then_inc(spare_done.sem, 1)
                for k in range(TILES):
                    yield 3 + 4 * k
                    gather(k)
                yield STATE0 + 4
                pool.wait_ge(*delta_ready(g, 2))
                pool.tensor_tensor(du[:, 1, :], delta[:, 1, :], u[:, 1, :], ALU.mult).then_inc(du_b_ready.sem, 1)
                for d in range(2):
                    for n in range(STATES):
                        k = d * STATES + n
                        yield STATE0 + STATE_DT * k + 2.5
                        if n == 0:
                            pool.wait_ge(*acc_init(g, d + 1))
                        pool.wait_ge(*p_done(g, k + 1))
                        if n:
                            pool.wait_ge(*acc_done(g, k))
                        pool.tensor_tensor(acc[:, d, :], acc[:, d, :], pC[:, k % RING, :], ALU.add
                                           ).then_inc(acc_done.sem, 1)

            def experts(g):
                yield 4.5
                root(g, 1, stR)
                normalise(g, 1, xR[:, :], xcR[:, :], stR).then_inc(xm_ready.sem, 1)
                yield 10
                pool.wait_ge(*xm_ready(g, 1))
                pool.tensor_tensor(hR[:, :], hR[:, :], xR[:, :], ALU.add).then_inc(hm_ready.sem, 1)
                yield PREP0 + 4
                root(g, 2, stR)
                normalise(g, 2, xR[:, :], xcR[:, :], stR).then_inc(xa_ready.sem, 1)
                yield PREP0 + 8
                pool.wait_ge(*xa_ready(g, 1))
                normalise_again(g, 2, xnR[:, :], xR[:, :], stR).then_inc(xaa_ready.sem, 1)
                yield PREP0 + 9
                pool.tensor_tensor(hR[:, :], hR[:, :], xR[:, :], ALU.add).then_inc(hR_done.sem, 1)

            def attention(g):
                yield 0
                pool.wait_ge(*pjV_done(g, 4))
                for w in range(32):
                    sb_, a, r = w // 8, w // 4 % 2, w % 4
                    s, b = divmod(sb_, 2)
                    h = 4 * b + r
                    yield ATT0 + ATT_DT * w + 3.2
                    pool.wait_ge(*exp_done(g, 2 * w + 2))
                    if w >= RING_S:
                        pool.wait_ge(*ot_done(g, w - RING_S + 1))
                    pool.tensor_tensor(rinv[:, w % RING_S, :], rsum[:, w % RING_S, :], C("mone"), ALU.pow
                                       ).then_inc(rinv_ready.sem, 1)
                    pool.wait_ge(*rinv_ready(g, w + 1))
                    v = vT[:, 2 * s + a, :].rearrange("p (c m) -> p c m", c=2)[:, :, h * HEAD_DIM:(h + 1) * HEAD_DIM]
                    pool.tensor_tensor(vs[:, w % RING_S, :, :], v, bcast(rinv[:, w % RING_S, :], HEAD_DIM), ALU.mult
                                       ).then_inc(vs_ready.sem, 1)
                yield BIN0 + 4
                root(g, 3, stS)
                normalise(g, 3, xS[:, :], xcS[:, :], stS).then_inc(xf_ready.sem, 1)

            iterations(pool.Fori, embed, scan, experts, attention)

        @block.tensor
        def _(pe):
            def flip(dst, src):
                for k in range(4):
                    i = pe.transpose(dst[:, k * P:(k + 1) * P], src[:, k * P:(k + 1) * P], ident)
                return i

            def mm(dst, lhsT, rhs, start=True, stop=True):
                return pe.matmul(dst, lhsT, rhs, start=start, stop=stop)

            def embed(g):
                yield EMB0 + 13.5
                pe.wait_ge(*xn_ready(g, 1))
                flip(eb[0], xnM).then_inc(xnT_ready.sem, 1)
                yield EMB0 + 16.5
                pe.wait_ge(*xnF_ready(g, 1))
                mm(eb[1], C("Wp"), xnF).then_inc(z1p_ready.sem, 1)

            def scan(g):
                for d in range(2):
                    yield 1 + d
                    if d == 0:
                        pe.wait_ge(*z1_ready(g, 1))
                        if not_first(g):
                            pe.wait_ge(*h1_ready(g - 1, 1))
                    mm(mb[d], C("Wc", d, 128), z1N[:, :]).then_inc(upre_ready.sem, 1)
                for d in range(2):
                    yield 9 + 5 * d
                    if d:
                        pe.wait_ge(*r1_ready(g, 1))
                    else:
                        pe.wait_ge(*u_ready(g, 2))
                    for j in range(2):
                        i = mm(mb[j][0:96, :], C("Wx", 2 * d + j, 96), u[:, d, :])
                    i.then_inc(xp_ready.sem, 1)
                for d in range(2):
                    yield 18.5 + d
                    pe.wait_ge(*r1_ready(g, 2))
                    mm(mb[d], Wdt[:, d, :], u[:, d, :]).then_inc(dpre_ready.sem, 1)
                for k in range(2 * STATES):
                    d, n = divmod(k, STATES)
                    yield STATE0 + STATE_DT * k - (2.4 if k else 1)
                    if k == 0:
                        pe.wait_ge(*delta_ready(g, 2))
                    else:
                        pe.wait_ge(*bx_done(g, k))
                    if n == 0:
                        pe.wait_ge(*sx_ready(g, d + 1))
                    mm(mb[0], sel[:, n, :], SX[:, d, 0:N]).then_inc(b_ready.sem, 1)
                    yield STATE0 + STATE_DT * k
                    if k:
                        pe.wait_ge(*p_done(g, k))
                    mm(mb[1], sel[:, n, :], SX[:, d, N:2 * N]).then_inc(c_ready.sem, 1)
                yield TAIL0 + 3
                pe.wait_ge(*m_ready(g, 1))
                flip(mb[0], mF).then_inc(mT_ready.sem, 1)

            def experts(g):
                def hidden(v):
                    if v == 1:
                        pe.wait_ge(*ls_ready(g, 1))
                    if v >= 2:
                        pe.wait_ge(*ge_ready(g, v - 1))
                    mm(eb[v % 2], C("W1", v, 128), aF[:, :]).then_inc(hp_ready.sem, 1)

                def spread(v):
                    ep, s = divmod(v, 2)
                    if v:
                        pe.wait_ge(*gg_ready(g, v))
                    else:
                        pe.wait_ge(*cT_ready(g, 1))
                    for k in range(4):
                        for e in range(2):
                            at = k * 16 + s * 8 + ep * 2 + e
                            i = mm(eb[0][64 * e:64 * e + 64, k * P:(k + 1) * P],
                                   comb[:, at:at + 1].to_broadcast([P, 64]), ident)
                    i.then_inc(cb_ready.sem, 1)

                def expert_out(v):
                    ep, s = divmod(v, 2)
                    pe.wait_ge(*gg_ready(g, v + 1))
                    mm(eb[1][64 * s:64 * s + 64, :], C("W2", ep, 64), ge[:, v, :], False, ep == 3
                       ).then_inc(mo_mm.sem, 1)

                yield 9
                pe.wait_ge(*xm_ready(g, 1))
                flip(eb[0], xR[:, :]).then_inc(xmT_ready.sem, 1)
                yield 12
                pe.wait_ge(*xmF_ready(g, 1))
                for k in range(4):
                    i = mm(eb[1][:, k * 16:(k + 1) * 16], aF[:, k * P:(k + 1) * P], C("router"))
                i.then_inc(lg_ready.sem, 1)
                hidden(0)
                for v in range(1, 8):
                    yield 14.8 + 0.3 * v
                    hidden(v)
                yield 24
                pe.wait_ge(*comb_ready(g, 1))
                pe.wait_ge(*ge_ready(g, 8))
                for k in range(4):
                    i = mm(eb[0][0:16, k * P:(k + 1) * P], comb[:, k * 16:(k + 1) * 16], ident)
                i.then_inc(cTp_ready.sem, 1)
                yield 26
                spread(0)
                for s in range(2):
                    mm(eb[1][64 * s:64 * s + 64, :], C("b2", s, 64, 16), cT, True, False)
                for v in range(1, 9):
                    yield 26 + 3 * v
                    if v < 8:
                        spread(v)
                    expert_out(v - 1)
                yield 54
                pe.wait_ge(*moF_ready(g, 1))
                flip(eb[0], aF[:, :]).then_inc(moT_ready.sem, 1)
                yield PREP0 + 8
                pe.wait_ge(*xa_ready(g, 1))
                flip(eb[0], xR[:, :]).then_inc(xaT_ready.sem, 1)
                yield PREP0 + 13
                pe.wait_ge(*xaa_ready(g, 1))
                flip(eb[1], xnR[:, :]).then_inc(xaT_ready.sem, 1)
                for w in range(16):
                    kind, i = divmod(w, 4)
                    yield (PREP0 + 17 if w < 12 else PREP0 + 23) + 1.3 * w
                    if w == 0:
                        pe.wait_ge(*xaF_ready(g, 2))
                    if w >= 2:
                        if w - 2 < 8:
                            pe.wait_ge(*pjA_done(g, w - 1))
                        elif w - 2 < 12:
                            pe.wait_ge(*pjV_done(g, w - 9))
                        else:
                            pe.wait_ge(*pjA_done(g, w - 5))
                    bank = eb[w % 2]
                    if kind != 2:
                        m = mm(bank, C({0: "Wq", 1: "Wk", 3: "Wg"}[kind], i, 128), (aF if kind == 3 else nF)[:, :])
                    else:
                        s, a = divmod(i, 2)
                        for c in range(2):
                            at = (2 * a + c) * P
                            m = mm(bank[:, c * SEQ:(c + 1) * SEQ], nF[:, at:at + P], C("Wv", s, SEQ))
                    m.then_inc(pj_ready.sem, 1)

            def attention(g):
                def scores(w):
                    sb_, a, r = w // 8, w // 4 % 2, w % 4
                    if w >= 3:
                        pe.wait_ge(*exp_done(g, 2 * (w - 2)))
                    for c in range(2):
                        at = a * SEQ + c * P
                        m = mm(bb[w % 3][:, c * SEQ:(c + 1) * SEQ], qF[:, sb_, at:at + P],
                               kz[:, 4 * sb_ + r, a * SEQ:(a + 1) * SEQ])
                    m.then_inc(sc_ready.sem, 1)

                def weighted(w):
                    sb_, a, r = w // 8, w // 4 % 2, w % 4
                    if w % 8 == 0 and sb_:
                        pe.wait_ge(*og_ready(g, sb_))
                    pe.wait_ge(*vs_ready(g, w + 1))
                    for c in range(2):
                        m = mm(bb[3][32 * r:32 * r + 32, a * SEQ:(a + 1) * SEQ], vs[:, w % RING_S, c, :],
                               prob[:, w % RING_S, c, :], c == 0, c == 1)
                    m.then_inc(ot_done.sem, 1)

                for w in range(35):
                    yield ATT0 + ATT_DT * w
                    if w == 0:
                        pe.wait_ge(*kz_landed(g, 256))
                        pe.wait_ge(*pjA_done(g, 12))
                        if not_first(g):
                            pe.wait_ge(*out_ready(g - 1, 1))
                    if w < 32:
                        scores(w)
                    yield ATT0 + ATT_DT * w + 0.5
                    if w >= 3:
                        weighted(w - 3)
                yield ATT1 + 2
                for i in range(4):
                    s, b = divmod(i, 2)
                    pe.wait_ge(*og_ready(g, i + 1))
                    m = mm(bb[0][64 * s:64 * s + 64, :], half_Wf[:, b, :], og[:, i, :], b == 0, b == 1)
                m.then_inc(fo_ready.sem, 1)
                yield ATT1 + 6
                pe.wait_ge(*foF_ready(g, 1))
                flip(bb[1], aS[:, :]).then_inc(foT_ready.sem, 1)
                yield BIN0 + 9
                pe.wait_ge(*xf_ready(g, 1))
                flip(bb[0], xS[:, :]).then_inc(xfT_ready.sem, 1)
                yield BIN0 + 12
                pe.wait_ge(*xfF_ready(g, 2))
                mm(bb[1][0:96, :], C("proj"), aS[:, :]).then_inc(gp_ready.sem, 1)

                def expand(w):
                    if w >= 3:
                        pe.wait_ge(*sg_ready(g, w - 2))
                    o = 16 * (w % 4) + w // 4
                    mm(bb[w % 3], Wt[:, o, :], G).then_inc(w_ready.sem, 1)

                def reduce(w):
                    q, j = w % 4, w // 4
                    pe.wait_ge(*zz_ready(g, w + 1))
                    mm(bb[3][32 * q:32 * q + 32, :], ones_w[:, j, :], sg[:, w % RING_S, :], j == 0, j == 15
                       ).then_inc(red_done.sem, 1)

                for w in range(D + 3):
                    yield BIN0 + 15 + BIN_DT * w
                    if w == 0:
                        pe.wait_ge(*G_ready(g, 1))
                        pe.wait_ge(w_split.sem, W_SPLIT)
                    if w < D:
                        expand(w)
                    if w >= 3:
                        reduce(w - 3)
                yield END + 1
                pe.wait_ge(*yF_ready(g, 1))
                for k in range(4):
                    i = mm(bb[0][:, k * P:(k + 1) * P], aS[:, k * P:(k + 1) * P], C("perm"))
                i.then_inc(yT_ready.sem, 1)

            pe.wait_ge(loaded.sem, 16 * LOADS)
            mm(mb[0][:, 0:P], C("dt_in", 0, 128, 32), C("dt_out", 0, 128, 32))
            mm(mb[1][:, 0:P], C("dt_in_b", 0, 128, 32), C("dt_out", 1, 128, 32)).then_inc(prepared.sem, 1)
            pe.wait_ge(prepared.sem, PREPARED)
            iterations(pe.Fori, embed, scan, experts, attention)

        @block.scalar
        def _(act):
            def square(g, i, dst, src):
                act.wait_ge(*ln_xc[i](g, 1))
                act.activation(dst, src, ACT.Square, scale=D ** -0.5).then_inc(ln_sq[i].sem, 1)

            def softplus_log(g, i):
                act.wait_ge(*um_ready(g, i + 1))
                act.activation(um[:, i % 2, :], um[:, i % 2, :], ACT.Exp).then_inc(se_ready.sem, 1)
                act.wait_ge(*se_ready(g, i + 1))
                act.activation(um[:, i % 2, :], um[:, i % 2, :], ACT.Ln, bias=1.0).then_inc(sl_ready.sem, 1)

            def embed(g):
                yield EMB0 + 2.5
                if not isinstance(g, int) or g > 1:
                    act.wait_ge(*hR_done(g - 2, 1))
                square(g, 0, sqM, xcM)
                yield EMB0 + 15
                act.wait_ge(*xnT_ready(g, 1))
                act.activation(xnF, eb[0], ACT.Identity, bias=C("ln_b"), scale=C("ln_g")
                               ).then_inc(xnF_ready.sem, 1)
                yield EMB0 + 18
                act.wait_ge(*z1p_ready(g, 1))
                if not_first(g):
                    act.wait_ge(*z1_moved(g - 1, 1))
                act.activation(z1N[:, :], eb[1], ACT.Identity, bias=C("bp")).then_inc(z1_ready.sem, 1)

            def scan(g):
                yield 0
                act.preload_act_table_set("natural_log_exp_and_others")
                for d in range(2):
                    yield 4.5 + 1.5 * d
                    softplus_log(g, d)
                for d in range(2):
                    yield 10.5 + 5 * d
                    act.wait_ge(*xp_ready(g, d + 1))
                    for j in range(2):
                        i = act.activation(hi[:, j * N:(j + 1) * N], mb[j][0:96, :], ACT.Copy)
                    i.then_inc(hi_ready.sem, 1)
                    yield 13.5 + 5 * d
                    act.wait_ge(*r1_ready(g, d + 1))
                    act.activation(mid, r1, ACT.Copy).then_inc(mid_ready.sem, 1)
                for d in range(2):
                    yield 21 + 1.5 * d
                    softplus_log(g, 2 + d)
                for k in range(2 * STATES):
                    d, n = divmod(k, STATES)
                    yield STATE0 + STATE_DT * k - 2
                    if n == 0:
                        act.wait_ge(*delta_ready(g, d + 1))
                    if n >= RING:
                        act.wait_ge(*h_done(g, k - RING + 1))
                    cols = slice(1, SEQ) if d == 0 else slice(0, SEQ - 1)
                    src = delta[:, d, :].rearrange("p (a t) -> p a t", a=2)[:, :, cols]
                    dst = dA[:, d, n % RING, :].rearrange("p (a t) -> p a t", a=2)[:, :, cols]
                    act.activation(dst, src, ACT.Exp, scale=negA[:, k:k + 1]).then_inc(dA_ready.sem, 1)
                yield TAIL0
                act.wait_ge(*acc_done(g, 2 * STATES))
                for d, src in enumerate((acc[:, 0, :], acc[:, 1, :], z1[:, :])):
                    act.activation(th[:, d, :], src, ACT.Tanh, scale=0.5).then_inc(th_ready.sem, 1)

            def experts(g):
                yield 2.5
                act.wait_ge(*hN_ready(g + 1, 1))
                square(g, 1, sqR[:, :], xcR[:, :])
                yield 10.5
                act.wait_ge(*xmT_ready(g, 1))
                act.activation(aF[:, :], eb[0], ACT.Copy).then_inc(xmF_ready.sem, 1)

                def hidden():
                    for v in range(8):
                        act.wait_ge(*hp_ready(g, v + 1))
                        act.activation(ge[:, v, :], eb[v % 2], ACT.Gelu, bias=C("b1", v // 2, 1)
                                       ).then_inc(ge_ready.sem, 1)
                    act.preload_act_table_set("natural_log_exp_and_others")

                yield 14
                act.wait_ge(*ls_ready(g, 1))
                act.activation(rt[:, 1, :], rt[:, 0, :], ACT.Exp).then_inc(le_ready.sem, 1)
                yield 15.5
                if not_first(g):
                    act.wait_ge(*kz_landed(g - 1, 256))
                hidden()
                yield 53
                act.wait_ge(*mo_mm(g, 8))
                act.activation(aF[:, :], eb[1], ACT.Copy).then_inc(moF_ready.sem, 1)
                yield PREP0 + 2
                square(g, 2, sqR[:, :], xcR[:, :])
                yield PREP0 + 9.5
                act.wait_ge(*xaT_ready(g, 1))
                act.activation(aF[:, :], eb[0], ACT.Copy).then_inc(xaF_ready.sem, 1)
                yield PREP0 + 14.5
                act.wait_ge(*xaT_ready(g, 2))
                act.activation(nF[:, :], eb[1], ACT.Identity, bias=C("beta"), scale=C("gamma")
                               ).then_inc(xaF_ready.sem, 1)
                for w in (*range(8), *range(12, 16)):
                    kind, i = divmod(w, 4)
                    yield (PREP0 + 18 if w < 12 else PREP0 + 24) + 1.3 * w
                    act.wait_ge(*pj_ready(g, w + 1))
                    if w == 0 and not_first(g):
                        act.wait_ge(*sc_ready(g - 1, 32))
                    if w == 12 and not_first(g):
                        act.wait_ge(*fo_ready(g - 1, 1))
                    if kind == 0:
                        m = act.activation(qF[:, i, :], eb[w % 2], ACT.Copy, scale=HEAD_DIM ** -0.5)
                    elif kind == 1:
                        m = act.activation(kF[:, i, :], eb[w % 2], ACT.Copy)
                    else:
                        m = act.activation(thg[:, i, :], eb[w % 2], ACT.Tanh, bias=half_bg[:, i % 2:i % 2 + 1],
                                           scale=0.5)
                    m.then_inc(pjA_done.sem, 1)

            def attention(g):
                for w in range(32):
                    yield ATT0 + ATT_DT * w + 2
                    act.wait_ge(*nmx_ready(g, w + 1))
                    if w >= RING_S:
                        act.wait_ge(*ot_done(g, w - RING_S + 1))
                    for c in range(2):
                        act.activation(prob[:, w % RING_S, c, :], bb[w % 3][:, c * SEQ:(c + 1) * SEQ], ACT.Exp,
                                       bias=nmx[:, w % RING_S, c:c + 1], accum_out=rsum[:, w % RING_S, c:c + 1]
                                       ).then_inc(exp_done.sem, 1)
                yield ATT1 + 4
                act.wait_ge(*fo_ready(g, 1))
                act.activation(aS[:, :], bb[0], ACT.Identity, bias=C("bf")).then_inc(foF_ready.sem, 1)
                yield BIN0 + 2
                square(g, 3, sqS[:, :], xcS[:, :])
                yield BIN0 + 10.5
                act.wait_ge(*xfT_ready(g, 1))
                act.activation(aS[:, :], bb[0], ACT.Copy).then_inc(xfF_ready.sem, 1)
                act.activation(xb, bb[0], ACT.Sign).then_inc(xfF_ready.sem, 1)
                for w in range(D):
                    yield BIN0 + 15.5 + BIN_DT * w
                    act.wait_ge(*w_ready(g, w + 1))
                    if w >= RING_S:
                        act.wait_ge(*red_done(g, w - RING_S + 1))
                    act.activation(sg[:, w % RING_S, :], bb[w % 3], ACT.Sign).then_inc(sg_ready.sem, 1)
                yield END
                act.wait_ge(*red_done(g, D))
                act.activation(aS[:, :], bb[3], ACT.Identity, bias=0.0, scale=C("scale")).then_inc(yF_ready.sem, 1)

            act.wait_ge(loaded.sem, 16 * LOADS)
            act.activation(negA[:, :], C("Alog"), ACT.Exp).then_inc(prepared.sem, 1)
            act.wait_ge(prepared.sem, PREPARED)
            iterations(act.Fori, embed, scan, experts, attention)

        @block.vector
        def _(dve):
            tt, ts, stt, red = dve.tensor_tensor, dve.tensor_scalar, dve.scalar_tensor_tensor, dve.tensor_reduce
            steps = {}

            def link(chain, g, ins):
                steps[chain] = steps.get(chain, 0) % chain.per + 1
                ins.then_inc(chain.sem, 1)
                dve.wait_ge(*chain(g, steps[chain]))

            def tiles(ap):
                return ap.rearrange("p (k d) -> p k d", k=TILES)

            def centre(chain, g, i, h, xc, st):
                link(chain, g, red(st[:, 0, :], tiles(h), AX.X, ALU.add))
                stt(tiles(xc), bcast(st[:, 0, :], D), -1.0 / D, tiles(h), ALU.mult, ALU.add).then_inc(ln_xc[i].sem, 1)

            def square_sum(g, i, sq, st):
                dve.wait_ge(*ln_sq[i](g, 1))
                red(st[:, 1, :], tiles(sq), AX.X, ALU.add).then_inc(ln_var[i].sem, 1)



            def clip(g, i, x, src, bias):
                ts(x, src, bias, None, ALU.add).then_inc(lin_ready.sem, 1)
                dve.wait_ge(*lin_ready(g, i + 1))
                ts(um[:, i % 2, :], x, SOFTPLUS_CAP, None, ALU.min).then_inc(um_ready.sem, 1)

            def softplus(g, i, x):
                dve.wait_ge(*sl_ready(g, i + 1))
                return tt(x, x, um[:, i % 2, :], ALU.max)

            def embed(g):
                yield EMB0
                dve.wait_ge(*emb_landed(g, 16 * TILES))
                tt(hN[:, :], hN[:, :], C("pe"), ALU.add).then_inc(pe_added.sem, 1)
                yield EMB0 + 1
                dve.wait_ge(*pe_added(g, 1))
                centre(chain_0, g, 0, hN[:, :], xcM, stM)
                yield EMB0 + 4
                square_sum(g, 0, sqM, stM)

            def scan(g):
                def weigh_b(k):
                    d = k // STATES
                    dve.wait_ge(*b_ready(g, k + 1))
                    dve.wait_ge(*(du_b_ready if d else du_f_ready)(g, 1))
                    tt(bx[:, k % 2, :], du[:, d, :], mb[0], ALU.mult).then_inc(bx_done.sem, 1)

                yield 0.5
                dve.wait_ge(*hN_ready(g, 1))
                if not_first(g):
                    dve.wait_ge(*h1_moved(g - 1, 1))
                dve.tensor_copy(hM[:, :], hN[:, :]).then_inc(h_moved.sem, 1)
                dve.wait_ge(*z1_ready(g, 1))
                dve.tensor_copy(z1[:, :], z1N[:, :]).then_inc(z1_moved.sem, 1)
                for d in range(2):
                    yield 3 + 1.5 * d
                    dve.wait_ge(*upre_ready(g, d + 1))
                    clip(g, d, u[:, d, :], mb[d], C("bc", d, 1))
                for d in range(2):
                    yield 6.5 + 1.5 * d
                    softplus(g, d, u[:, d, :]).then_inc(u_ready.sem, 1)
                dve.wait_ge(*u_ready(g, 2))
                for d in range(2):
                    yield 12 + 5 * d
                    dve.wait_ge(*hi_ready(g, d + 1))
                    if d:
                        dve.wait_ge(*sx_ready(g, 1))
                    for j in range(2):
                        i = stt(r1[:, j * N:(j + 1) * N], hi[:, j * N:(j + 1) * N], C("n1", rows=96),
                                mb[j][0:96, :], ALU.mult, ALU.add)
                    i.then_inc(r1_ready.sem, 1)
                    yield 15 + 5 * d
                    dve.wait_ge(*r1_ready(g, d + 1))
                    dve.wait_ge(*mid_ready(g, d + 1))
                    stt(SX[:, d, :], mid, C("n2", rows=96), r1, ALU.mult, ALU.add).then_inc(sx_ready.sem, 1)
                for d in range(2):
                    yield 20 + d
                    if d == 0:
                        dve.wait_ge(*sx_ready(g, 2))
                    dve.wait_ge(*dpre_ready(g, d + 1))
                    clip(g, 2 + d, delta[:, d, :], mb[d], C("bdt", d, 1))
                yield 22.5
                for d in range(2):
                    ts(acc[:, d, :], u[:, d, :], C("Dskip", d, 1), None, ALU.mult).then_inc(acc_init.sem, 1)
                for d in range(2):
                    yield 23.5 + d
                    softplus(g, 2 + d, delta[:, d, :]).then_inc(delta_ready.sem, 1)
                dve.wait_ge(*delta_ready(g, 1))
                tt(du[:, 0, :], delta[:, 0, :], u[:, 0, :], ALU.mult).then_inc(du_f_ready.sem, 1)
                yield STATE0
                weigh_b(0)
                for k in range(2 * STATES):
                    d, turn = k // STATES, slice(None, None, -1 if k >= STATES else 1)
                    yield STATE0 + STATE_DT * k + 0.5
                    dve.wait_ge(*dA_ready(g, k + 1))
                    dve.wait_ge(*bx_done(g, k + 1))
                    dve.tensor_tensor_scan(hs[:, k % 2, turn], dA[:, d, k % STATES % RING, turn], bx[:, k % 2, turn],
                                           0.0, ALU.mult, ALU.add).then_inc(h_done.sem, 1)
                    if k + 1 < 2 * STATES:
                        yield STATE0 + STATE_DT * k + 1
                        weigh_b(k + 1)
                    yield STATE0 + STATE_DT * k + 1.8
                    dve.wait_ge(*c_ready(g, k + 1))
                    dve.wait_ge(*h_done(g, k + 1))
                    if k >= RING:
                        dve.wait_ge(*acc_done(g, k - RING + 1))
                    tt(pC[:, k % RING, :], hs[:, k % 2, :], mb[1], ALU.mult).then_inc(p_done.sem, 1)
                yield TAIL0 + 2
                dve.wait_ge(*acc_done(g, 2 * STATES))
                dve.wait_ge(*th_ready(g, 3))
                dve.wait_ge(*z1_moved(g, 1))
                stt(sy[:, 0, :], th[:, 0, :], 1.0, acc[:, 0, :], ALU.add, ALU.mult)
                link(chain_m, g, stt(sy[:, 1, :], th[:, 1, :], 1.0, acc[:, 1, :], ALU.add, ALU.mult))
                stt(th[:, 2, :], th[:, 2, :], 1.0, z1[:, :], ALU.add, ALU.mult)
                link(chain_m, g, tt(sy[:, 0, :], sy[:, 0, :], sy[:, 1, :], ALU.add))
                stt(mF, sy[:, 0, :], 0.25, th[:, 2, :], ALU.mult, ALU.mult).then_inc(m_ready.sem, 1)
                yield TAIL0 + 5
                dve.wait_ge(*mT_ready(g, 1))
                dve.wait_ge(*h_moved(g, 1))
                tt(hM[:, :], hM[:, :], mb[0], ALU.add).then_inc(h1_ready.sem, 1)

            def experts(g):
                e8 = EXPERTS

                def t3(j):
                    return rt[:, j, :].rearrange("p (k e) -> p k e", e=e8)

                yield 0.2
                dve.wait_ge(*h1_ready(g, 1))
                if not_first(g):
                    dve.wait_ge(*hS_ready(g - 1, 1))
                dve.tensor_copy(hR[:, :], hM[:, :]).then_inc(h1_moved.sem, 1)
                yield 1
                dve.wait_ge(*h1_moved(g, 1))
                centre(chain_e, g, 1, hR[:, :], xcR[:, :], stR)
                yield 4
                square_sum(g, 1, sqR[:, :], stR)
                mx, sm, ri, m1, i1, m2, i2, dn, rd = (rs8[:, j, :] for j in range(9))
                logits = eb[1][:, 0:TILES * e8].rearrange("p (k e) -> p k e", e=e8)
                iota = C("iota").rearrange("p (k e) -> p k e", e=e8)
                yield 13
                dve.wait_ge(*lg_ready(g, 1))
                link(chain_e, g, red(mx, logits, AX.X, ALU.max))
                tt(t3(0), logits, bcast(mx, e8), ALU.subtract).then_inc(ls_ready.sem, 1)
                yield 16
                dve.wait_ge(*le_ready(g, 1))
                link(chain_e, g, red(sm, t3(1), AX.X, ALU.add))
                link(chain_e, g, dve.reciprocal(ri, sm))
                link(chain_e, g, tt(t3(2), t3(1), bcast(ri, e8), ALU.mult))
                for m, i, onehot, rest in ((m1, i1, 4, 6), (m2, i2, 5, None)):
                    yield 17 if rest else 19
                    probs = t3(2) if rest else t3(6)
                    link(chain_e, g, red(m, probs, AX.X, ALU.max))
                    link(chain_e, g, tt(t3(3), probs, bcast(m, e8), ALU.is_equal))
                    link(chain_e, g, stt(t3(3), t3(3), -float(e8), iota, ALU.mult, ALU.add))
                    yield 18 if rest else 20
                    link(chain_e, g, red(i, t3(3), AX.X, ALU.min))
                    link(chain_e, g, stt(t3(onehot), iota, -float(e8), bcast(i, e8), ALU.add, ALU.is_equal))
                    if rest:
                        link(chain_e, g, stt(t3(rest), t3(onehot), -2.0, t3(2), ALU.mult, ALU.add))
                yield 21
                link(chain_e, g, tt(dn, m1, m2, ALU.add))
                link(chain_e, g, ts(dn, dn, 1e-12, None, ALU.max))
                link(chain_e, g, dve.reciprocal(rd, dn))
                yield 22
                tt(t3(4), t3(4), bcast(m1, e8), ALU.mult)
                link(chain_e, g, tt(t3(5), t3(5), bcast(m2, e8), ALU.mult))
                link(chain_e, g, tt(t3(4), t3(4), t3(5), ALU.add))
                tt(comb[:, :].rearrange("p (k e) -> p k e", e=e8), t3(4), bcast(rd, e8), ALU.mult
                   ).then_inc(comb_ready.sem, 1)
                yield 25
                dve.wait_ge(*cTp_ready(g, 1))
                dve.tensor_copy(cT, eb[0][0:16, :]).then_inc(cT_ready.sem, 1)
                for v in range(8):
                    yield 28 + 3 * v
                    dve.wait_ge(*ge_ready(g, v + 1))
                    dve.wait_ge(*cb_ready(g, v + 1))
                    tt(ge[:, v, :], ge[:, v, :], eb[0], ALU.mult).then_inc(gg_ready.sem, 1)
                yield PREP0
                dve.wait_ge(*moT_ready(g, 1))
                dve.wait_ge(*hm_ready(g, 1))
                link(chain_e, g, tt(hR[:, :], hR[:, :], eb[0], ALU.add))
                centre(chain_e, g, 2, hR[:, :], xcR[:, :], stR)
                yield PREP0 + 3.5
                square_sum(g, 2, sqR[:, :], stR)
                for i in range(4):
                    yield PREP0 + 18 + 1.3 * (8 + i)
                    dve.wait_ge(*pj_ready(g, 8 + i + 1))
                    if i == 0 and not_first(g):
                        dve.wait_ge(*vs_ready(g - 1, 32))
                    dve.tensor_copy(vT[:, i, :], eb[i % 2]).then_inc(pjV_done.sem, 1)

            def attention(g):
                def row_max(w):
                    dve.wait_ge(*sc_ready(g, w + 1))
                    red(nmx[:, w % RING_S, :], bb[w % 3].rearrange("p (c t) -> p c t", c=2), AX.X, ALU.max,
                        negate=True).then_inc(nmx_ready.sem, 1)


                yield 0
                dve.wait_ge(*hR_done(g, 1))
                if not_first(g):
                    dve.wait_ge(*stored(g, 0))
                dve.tensor_copy(hS[:, :], hR[:, :]).then_inc(hS_ready.sem, 1)
                for w in range(33):
                    if w < 32:
                        yield ATT0 + ATT_DT * w + 1.2
                        row_max(w)
                    if w >= 8 and w % 8 == 0:
                        i = w // 8 - 1
                        yield ATT0 + ATT_DT * (w - 1) + 5.6
                        dve.wait_ge(*ot_done(g, 8 * i + 8))
                        dve.wait_ge(*pjA_done(g, 8 + i + 1))
                        stt(og[:, i, :], thg[:, i, :], 1.0, bb[3], ALU.add, ALU.mult).then_inc(og_ready.sem, 1)
                yield BIN0
                dve.wait_ge(*foT_ready(g, 1))
                link(chain_s, g, tt(hS[:, :], hS[:, :], bb[1], ALU.add))
                centre(chain_s, g, 3, hS[:, :], xcS[:, :], stS)
                yield BIN0 + 3.5
                square_sum(g, 3, sqS[:, :], stS)
                yield BIN0 + 13.5
                dve.wait_ge(*gp_ready(g, 1))
                ts(G, bb[1][0:96, :], C("pb", rows=96), 0.0, ALU.add, ALU.is_gt).then_inc(G_ready.sem, 1)
                for w in range(D):
                    yield BIN0 + 16 + BIN_DT * w
                    if w == 0:
                        dve.wait_ge(*xfF_ready(g, 2))
                    dve.wait_ge(*sg_ready(g, w + 1))
                    tt(sg[:, w % RING_S, :], sg[:, w % RING_S, :], xb, ALU.mult).then_inc(zz_ready.sem, 1)
                yield END + 2
                dve.wait_ge(*yT_ready(g, 1))
                tt(outT[:, :], hS[:, :], bb[0], ALU.add).then_inc(out_ready.sem, 1)

            dve.wait_ge(loaded.sem, 16 * LOADS)
            dve.memset(dA[:, :, :, :], 0.0).then_inc(prepared.sem, 1)
            ts(half_bg[:, :], C("bg"), 0.5, None, ALU.mult).then_inc(prepared.sem, 1)
            ts(half_Wf[:, :, :].rearrange("p b d -> p (b d)"), C("Wf"), 0.5, None, ALU.mult).then_inc(prepared.sem, 1)
            dve.wait_ge(prepared.sem, 3 + 1 + 1)
            ts(negA[:, :], negA[:, :], -1.0, None, ALU.mult).then_inc(prepared.sem, 1)
            for d in range(2):
                dve.tensor_copy(Wdt[:, d, :], mb[d][:, 0:P]).then_inc(prepared.sem, 1)
            dve.wait_ge(prepared.sem, PREPARED)

            def split_weights():
                for q in range(8):
                    w, n, slot = kz[0:96, q, :], 6 * q, 5 + 12 * q
                    yield slot
                    if q == 0:
                        dve.wait_ge(w_loaded.sem, 16)
                    else:
                        dve.wait_ge(w_split.sem, n)
                    dve.tensor_copy(sg[0:96, 0, :], w).then_inc(w_split.sem, 1)
                    yield slot + 2
                    dve.wait_ge(w_split.sem, n + 1)
                    stt(w, sg[0:96, 0, :], C("w_n1", rows=96), w, ALU.mult, ALU.add).then_inc(w_split.sem, 1)
                    yield slot + 4
                    dve.wait_ge(w_split.sem, n + 2)
                    dve.tensor_copy(sg[0:96, 1, :], w).then_inc(w_split.sem, 1)
                    yield slot + 6
                    dve.wait_ge(w_split.sem, n + 3)
                    stt(w, sg[0:96, 1, :], C("w_n2", rows=96), w, ALU.mult, ALU.add).then_inc(w_split.sem, 1)
                    for s in range(2):
                        yield slot + 8 + 2 * s
                        dve.wait_ge(w_split.sem, n + 4)
                        ts(Wt[:, 8 * q:8 * q + 8, s * D:(s + 1) * D], w.rearrange("p (o i) -> p o i", i=D),
                           C("w_s", s, 1, 96), None, ALU.mult).then_inc(w_split.sem, 1)
                yield 5 + 12 * 8
                dve.wait_ge(w_split.sem, W_SPLIT - 1)
                dve.memset(kz[:, :, :], 0.0).then_inc(w_split.sem, 1)

            iterations(dve.Fori, embed, scan, experts, attention, split_weights())
            assert all(steps[c] == c.per for c in steps), {k: v for k, v in zip("mes", steps.values())}


def layout(inputs):
    import numpy as np

    f = np.float32
    c = np.zeros((P, NCONST), f)

    def at(name, i=0, w=None):
        a, width = COL[name]
        w = width if w is None else w
        return c[:, a + i * w:a + (i + 1) * w]

    L0 = {k[len("L0_attn_"):]: np.asarray(v) for k, v in inputs.items() if k.startswith("L0_attn_")}
    E0 = {k[len("L0_ffn_"):]: np.asarray(v) for k, v in inputs.items() if k.startswith("L0_ffn_")}
    L1 = {k[len("L1_attn_"):]: np.asarray(v) for k, v in inputs.items() if k.startswith("L1_attn_")}
    E1 = {k[len("L1_ffn_"):]: np.asarray(v) for k, v in inputs.items() if k.startswith("L1_ffn_")}
    at("ident")[:] = np.eye(P)
    for s in range(2):
        r = slice(s * D, s * D + D)
        at("Wp")[r, r] = L0["Wp"]
        for d, x in enumerate("fb"):
            at("Wc", d, 128)[r, r] = L0["Wc" + x].T
            for j in range(2):
                for part in range(3):
                    k = part * 32 + s * 16
                    at("Wx", 2 * d + j, 96)[r, k:k + 16] = L0["Wdbc_" + x][:, 16 + 16 * j:32 + 16 * j]
            rr = slice(s * 16, s * 16 + 16)
            at("dt_in" if d == 0 else "dt_in_b")[rr, r] = L0["Wdbc_" + x][:, :16].T
            at("dt_out", d, 128)[rr, r] = L0["Wdt_" + x]
            at("bc")[r, d] = L0["bc" + x]
            at("bdt")[r, d] = L0["bdt_" + x]
            at("Dskip")[r, d] = L0["D_" + x]
            at("Alog", d, 16)[r] = L0["Alog_" + x]
        for name, v in (("ln_g", L0["ln_g"]), ("ln_b", L0["ln_b"]), ("bp", L0["bp"]), ("gamma", L1["ln_gamma"]),
                        ("beta", L1["ln_beta"]), ("bf", L1["b_final"])):
            at(name)[r, 0] = v
        for ep in range(4):
            for e in range(2):
                at("W1", 2 * ep + s, 128)[r, e * D:(e + 1) * D] = E0["w1"][2 * ep + e]
        at("b2")[s * 8:s * 8 + 8, r] = E0["b2"]
        at("router")[r, s * 8:s * 8 + 8] = E0["router_w"].T
        for b in range(2):
            m = slice(b * P, b * P + P)
            at("Wq", 2 * s + b, 128)[r] = L1["W_qkv"][m].T
            at("Wk", 2 * s + b, 128)[r] = L1["W_qkv"][256:][m].T
            at("Wg", 2 * s + b, 128)[r] = L1["W_gate"][m].T
        at("Wv", s, 256)[r] = L1["W_qkv"][512:].T
        for part in range(3):
            k = part * 16 + s * 8
            at("proj")[r, k:k + 8] = E1["proj_w"].T
            at("pb")[k:k + 8, 0] = E1["proj_b"]
            at("w_s")[k:k + 8, s] = 1
        for q in range(4):
            k = q * 32 + s * 16
            at("scale")[k:k + 16, 0] = E1["scale"][0, 0, q * 16:(q + 1) * 16]
            for o in range(16):
                at("perm")[k + o, s * D + q * 16 + o] = 1
    at("pb")[48:96] = -1
    for ep in range(4):
        for e in range(2):
            at("W2", ep, 64)[e * D:(e + 1) * D] = E0["w2"][2 * ep + e]
            at("b1")[e * D:(e + 1) * D, ep] = E0["b1"][2 * ep + e]
    for b in range(2):
        at("bg")[:, b] = L1["b_gate"][b * P:(b + 1) * P]
        at("Wf", b, 64)[:] = L1["W_final"][:, b * P:(b + 1) * P].T
    at("n1")[32:96] = -1
    at("n2")[64:96] = -1
    at("w_n1")[16:48] = -1
    at("w_n2")[32:48] = -1
    at("mhalf")[:] = -0.5
    at("mone")[:] = -1
    at("eps")[:] = EPS
    at("iota")[:] = np.tile(np.arange(EXPERTS, dtype=f), TILES)
    pos = np.arange(SEQ, dtype=f)[:, None]
    dim = np.arange(D)
    inv = np.power(f(10000.0), -((dim - dim % 2).astype(f) / f(D)), dtype=f)
    angle = (pos * inv).astype(f)
    pe = np.where(dim % 2 == 0, np.sin(angle), np.cos(angle)).astype(f)
    at("pe").reshape(P, 2, 2, 2, D)[:] = pe.reshape(2, P, D).transpose(1, 0, 2)[:, None, :, None, :]

    one = 0x3F80
    sel = np.zeros((96, STATES, P), np.uint16)
    for part in range(3):
        for s in range(2):
            for n in range(STATES):
                sel[part * 32 + s * 16 + n, n, s * D:(s + 1) * D] = one
    ones = np.zeros((P, 16, 32), np.uint16)
    for s in range(2):
        for j in range(16):
            ones[s * D:(s + 1) * D, j, s * 16 + j] = one
    w = np.zeros((96, 8, N), f)
    wt = E1["weight"][0].transpose(0, 2, 1).reshape(EXPERTS, 8, N)
    for k in range(6):
        w[k * 8:k * 8 + 8] = wt
    x = np.asarray(inputs["x"]).astype(np.int32)
    ids = np.zeros((P, (GROUPS + 1) * TILES), np.int32)
    ids[:, :GROUPS * TILES] = x.reshape(GROUPS, 2, 2, 2, P).transpose(4, 0, 1, 3, 2).reshape(P, -1)
    return {"table": np.ascontiguousarray(inputs["L0_tok_W"]), "ids": ids, "consts": c, "selectors": sel,
            "ones_sel": ones, "w_exp": w}


def kernel(**inputs):
    import numpy as np
    from concourse import bacc
    from concourse.bass_utils import run_bass_kernel_spmd

    nc = bacc.Bacc("TRN2", target_bir_lowering=False, num_devices=1)
    arrays = layout(inputs)
    args = [nc.dram_tensor(k, a.shape, mybir.dt.from_np(a.dtype), kind="ExternalInput").ap()
            for k, a in arrays.items()]
    args.append(nc.dram_tensor("out", (GROUPS * P, N), F32, kind="ExternalOutput").ap())
    build_tower(nc, *args)
    r = run_bass_kernel_spmd(nc, [arrays], core_ids=[0])
    got = np.asarray(r.results[0]["out"]).reshape(GROUPS, P, 2, 2, 2, D)
    return got.transpose(0, 2, 4, 3, 1, 5).reshape(BATCH, SEQ, D)
```
